# Optimizing a Trainium2 kernel written in Bass

```python
import numpy as np
import jax
import jax.numpy as jnp

def _softmax(x, axis=-1):
    return jax.nn.softmax(x, axis=axis)

def _gelu(x):
    return jax.nn.gelu(x, approximate=True)

def _silu(x):
    return jax.nn.silu(x)

def _sigmoid(x):
    return jax.nn.sigmoid(x)

def _layernorm(x, axis=-1, eps=1e-05):
    m = jnp.mean(x, axis=axis, keepdims=True)
    v = jnp.var(x, axis=axis, keepdims=True)
    return (x - m) / jnp.sqrt(v + eps)

def _scatter_add(tgt, idx, src, axis=0):
    return tgt.at[idx].add(src)

def _segment_sum(src, seg, n):
    return jax.ops.segment_sum(src, seg, n)
kernel_name = 'mk_seq_postln_d1_jaxref_r4_69a562'

def setup_inputs(seed: int=0):
    np.random.seed(seed)
    _w = jnp.asarray

    def _L0_attn_setup():
        import jax, jax.numpy as jnp
        import numpy as np
        B, L, D = (2, 512, 256)
        H, HD = (16, 64)
        LD = 64
        key = jax.random.key(seed)
        ks = jax.random.split(key, 6)
        s = lambda fan_in: 1.0 / np.sqrt(fan_in)
        x_bld = jax.random.normal(ks[0], (B, L, D), dtype=jnp.float32)
        Wq = jax.random.normal(ks[1], (D, H, HD), dtype=jnp.float32) * s(D)
        Wkv_down = jax.random.normal(ks[2], (D, LD), dtype=jnp.float32) * s(D)
        Wk_up = jax.random.normal(ks[3], (LD, H, HD), dtype=jnp.float32) * s(LD)
        Wv_up = jax.random.normal(ks[4], (LD, H, HD), dtype=jnp.float32) * s(LD)
        Wout = jax.random.normal(ks[5], (H, HD, D), dtype=jnp.float32) * s(H * HD)
        return {'x_bld': x_bld, 'Wq': Wq, 'Wkv_down': Wkv_down, 'Wk_up': Wk_up, 'Wv_up': Wv_up, 'Wout': Wout}
    _L0_attn_in = _L0_attn_setup()

    def _L0_ffn_setup():
        import math
        import jax, jax.numpy as jnp
        import numpy as np
        CAPACITY_FACTOR = 1.25
        key = jax.random.key(seed)
        ks = jax.random.split(key, 5)
        B, S, H, F, E = (4, 1024, 256, 256, 32)
        scale_in = 1.0 / math.sqrt(H)
        scale_mid = 1.0 / math.sqrt(F)
        return {'x': jax.random.normal(ks[0], (B, S, H), dtype=jnp.float32), 'w_router': jax.random.normal(ks[1], (H, E), dtype=jnp.float32) * scale_in, 'w_gate': jax.random.normal(ks[2], (E, H, F), dtype=jnp.float32) * scale_in, 'w_up': jax.random.normal(ks[3], (E, H, F), dtype=jnp.float32) * scale_in, 'w_down': jax.random.normal(ks[4], (E, F, H), dtype=jnp.float32) * scale_mid}
    _L0_ffn_in = _L0_ffn_setup()
    _d = {'L0_attn_x_bld': _L0_attn_in['x_bld'], 'L0_attn_Wq': _L0_attn_in['Wq'], 'L0_attn_Wkv_down': _L0_attn_in['Wkv_down'], 'L0_attn_Wk_up': _L0_attn_in['Wk_up'], 'L0_attn_Wv_up': _L0_attn_in['Wv_up'], 'L0_attn_Wout': _L0_attn_in['Wout'], 'L0_ffn_w_router': _L0_ffn_in['w_router'], 'L0_ffn_w_gate': _L0_ffn_in['w_gate'], 'L0_ffn_w_up': _L0_ffn_in['w_up'], 'L0_ffn_w_down': _L0_ffn_in['w_down']}
    _x0 = _d['L0_attn_x_bld']
    _d['L0_attn_x_bld'] = jax.random.normal(jax.random.fold_in(jax.random.key(seed), 1), (8, 1024, 256), dtype=_x0.dtype)
    del _x0
    return _d

def reference(L0_attn_x_bld, L0_attn_Wq, L0_attn_Wkv_down, L0_attn_Wk_up, L0_attn_Wv_up, L0_attn_Wout, L0_ffn_w_router, L0_ffn_w_gate, L0_ffn_w_up, L0_ffn_w_down):

    def _L0_attn_ref(x_bld, Wq, Wkv_down, Wk_up, Wv_up, Wout):
        import jax, jax.numpy as jnp
        import numpy as np
        B, L, D = (2, 512, 256)
        H, HD = (16, 64)
        LD = 64
        q_blhd = jnp.einsum('bld,dhk->blhk', x_bld, Wq)
        latent_bll = jnp.einsum('bld,dc->blc', x_bld, Wkv_down)
        k_blhd = jnp.einsum('blc,chk->blhk', latent_bll, Wk_up)
        v_blhd = jnp.einsum('blc,chk->blhk', latent_bll, Wv_up)
        attn = jnp.einsum('bqhd,bkhd->bhqk', q_blhd, k_blhd) / jnp.sqrt(jnp.asarray(HD, dtype=x_bld.dtype))
        l = x_bld.shape[1]
        mask = (jnp.arange(l)[None, :] <= jnp.arange(l)[:, None])[None, None]
        neg_inf = jnp.finfo(attn.dtype).min
        attn = jax.nn.softmax(jnp.where(mask, attn, neg_inf), axis=-1)
        y_blhd = jnp.einsum('bhqk,bkhd->bqhd', attn, v_blhd)
        return jnp.einsum('bqhd,hdo->bqo', y_blhd, Wout)

    def _L0_ffn_ref(x, w_router, w_gate, w_up, w_down):
        import math
        import jax, jax.numpy as jnp
        import numpy as np
        CAPACITY_FACTOR = 1.25
        B, S, H = x.shape
        E = w_gate.shape[0]
        T = B * S
        C = int(math.ceil(CAPACITY_FACTOR * T / E))
        xt = x.reshape(T, H)
        logits = xt @ w_router
        probs = jax.nn.softmax(logits, axis=-1)
        top1 = jnp.argmax(probs, axis=-1)
        gate = jnp.take_along_axis(probs, top1[:, None], axis=1)[:, 0]
        onehot = jax.nn.one_hot(top1, E, dtype=jnp.int32)
        pos = jnp.cumsum(onehot, axis=0)[jnp.arange(T), top1] - 1
        accepted = pos < C
        slot = jnp.where(accepted, top1 * C + pos, E * C)
        buf = jnp.zeros((E * C + 1, H), dtype=x.dtype).at[slot].set(xt)
        buf = buf[:E * C].reshape(E, C, H)
        g = jnp.einsum('ech,ehf->ecf', buf, w_gate)
        u = jnp.einsum('ech,ehf->ecf', buf, w_up)
        y = jnp.einsum('ecf,efh->ech', jax.nn.silu(g) * u, w_down)
        out_tok = y.reshape(E * C, H)[jnp.clip(slot, 0, E * C - 1)]
        out_tok = jnp.where(accepted[:, None], out_tok * gate[:, None], 0.0)
        return (xt + out_tok).reshape(B, S, H)
    x = L0_attn_x_bld
    x = _layernorm(x + _L0_attn_ref(x, L0_attn_Wq, L0_attn_Wkv_down, L0_attn_Wk_up, L0_attn_Wv_up, L0_attn_Wout), axis=-1)
    x = _layernorm(x + _L0_ffn_ref(x, L0_ffn_w_router, L0_ffn_w_gate, L0_ffn_w_up, L0_ffn_w_down), axis=-1)
    return x

_drawn_inputs = setup_inputs


def setup_inputs(seed=0):
    import zlib

    import numpy as np

    out = dict(_drawn_inputs(seed))
    spreads = {}
    factors = {}
    for name, (base, spread) in spreads.items():
        noise = np.random.default_rng([zlib.crc32(name.encode()), seed]).standard_normal(out[name].shape)
        drawn = base * np.exp(spread * noise) if base else spread * noise
        out[name] = jnp.asarray(drawn.astype(out[name].dtype))
    for name, factor in factors.items():
        out[name] = (out[name] * factor).astype(out[name].dtype)
    return out
```

```python
import math
from contextlib import ExitStack

import numpy as np

import concourse.bass as bass
from concourse import mybir

ALU = mybir.AluOpType
ACT = mybir.ActivationFunctionType
AX = mybir.AxisListType
F32 = mybir.dt.float32
F32R = mybir.dt.float32r
BF16 = mybir.dt.bfloat16
I32 = mybir.dt.int32

P = 128
BANK = 512
EPS = 1e-5
MASKED = -1e30
FAR = 2.0 ** 22


def build_layer(nc, x, Wq, Wkv, Wk_up, Wv_up, Wout, w_router, w_gate, w_up, w_down, out):
    B, L, D = x.shape
    _, H, HD = Wq.shape
    LD = Wkv.shape[1]
    E, _, F = w_gate.shape
    T = B * L
    C = int(math.ceil(1.25 * T / E))
    NT = L // P
    NPAIR = H // 2
    KD = D // P
    KF = F // P
    HPB = BANK // P
    assert HD == 64 and LD == 64 and KD == 2 and KF == 2 and NT == 8 and D == 256 and C <= BANK
    SLOTS = E * C
    BLOCKS = [(r, min(P, C - r)) for r in range(0, C, P)]
    NB = len(BLOCKS)

    slots_x = nc.dram_tensor("slots_x", [SLOTS, D], F32, kind="Internal").ap()
    slots_y = nc.dram_tensor("slots_y", [SLOTS, D], F32, kind="Internal").ap()
    x_tiles = x.rearrange("b (t p) d -> b p t d", p=P)
    out_tiles = out.rearrange("b (t p) d -> (b t) p d", p=P)

    with ExitStack() as ctx:
        def sb(name, shape, dt=F32, stack=ctx):
            return stack.enter_context(nc.sbuf_tensor(name, shape, dt))

        def sem(name):
            return ctx.enter_context(nc.semaphore(name))

        score_ps = [ctx.enter_context(nc.psum_tensor(f"score_ps{i}", [P, 2 * BANK], F32)) for i in range(2)]
        ring = [ctx.enter_context(nc.psum_tensor(f"ring{i}", [P, BANK], F32)) for i in range(2)]
        head_ps = [ctx.enter_context(nc.psum_tensor(f"head_ps{i}", [P, BANK], F32)) for i in range(2)]

        x1_all = sb("x1_all", [P, B * NT, D])
        gate_all = sb("gate_all", [P, B * NT])
        fetch_all = sb("fetch_all", [P, B * NT], I32)
        ident = sb("ident", [P, P])
        stat6 = sb("stat6", [P, 8, 6])
        mean_var = sb("mean_var", [P, 8, 2])
        var_eps = sb("var_eps", [P, 8])
        rstd = sb("rstd", [P, 8])
        minus_half = sb("minus_half", [P, 8])

        attn = ExitStack()
        ident_bf = sb("ident_bf", [P, P], BF16, attn)
        future_bf = sb("future_bf", [P, P], BF16, attn)
        before_bf = sb("before_bf", [P, P], BF16, attn)
        ones_bf = sb("ones_bf", [P, P], BF16, attn)
        expert_m = sb("expert_m", [P, E], F32, attn)
        expert_i = sb("expert_i", [P, E], I32, attn)
        x_in = sb("x_in", [P, NT, D], F32, attn)
        x_res = sb("x_res", [P, NT, D], F32, attn)
        xT = sb("xT", [P, KD, L], F32, attn)
        lat_hi = sb("lat_hi", [P, L], F32R, attn)
        lat_lo = sb("lat_lo", [P, L], F32R, attn)
        lat = sb("lat", [P, NT, LD], F32, attn)
        fold_q = sb("fold_q", [P, KD, (NPAIR + 1) * P], F32, attn)
        fold_stage = sb("fold_stage", [P, KD, P], F32, attn)
        fold_v = sb("fold_v", [P, NPAIR, D], F32, attn)
        q_hl = sb("q_hl", [P, 2, L], F32R, attn)
        probs = sb("probs", [P, 2, L], F32, attn)
        probsT = sb("probsT", [P, 2, L], F32, attn)
        negmax = sb("negmax", [P, 2 * NT], F32, attn)
        rowsum = sb("rowsum", [P, 2 * NT], F32, attn)
        rinv = sb("rinv", [P, 2 * NT], F32, attn)
        heads = sb("heads", [P, NT, P], F32, attn)
        headsT = sb("headsT", [P, NPAIR + 1, L], F32, attn)
        x1 = sb("x1", [P, NT, D], F32, attn)
        wkv2 = sb("wkv2", [P, KD, 2, LD], F32, attn)
        wr = sb("wr", [P, KD, E], F32, attn)
        logit = sb("logit", [P, NT, E], F32, attn)
        work_a = sb("work_a", [P, NT, E], F32, attn)
        work_b = sb("work_b", [P, NT, E], F32, attn)
        onehot = sb("onehot", [P, NT, E], BF16, attn)
        earlier = sb("earlier", [P, NT + 1, E], BF16, attn)
        rt = sb("rt", [P, 10, NT], F32, attn)
        send_idx = sb("send_idx", [P, NT], I32, attn)

        room = x1_all[:, :, :].rearrange("p t d -> p (t d)")
        if B * NT * D < 9728:
            room = sb("setup_room", [P, 9728], F32, attn)[:, :]
        at = [0]

        def carve(cols):
            at[0] += cols
            return room[:, at[0] - cols:at[0]]

        wq_in = carve(KD * H * HD).rearrange("p (k n) -> p k n", k=KD)
        wqT = carve(NPAIR * D)
        wk_in = carve(H * HD)
        wv_in = carve(H * HD)
        wkT = carve(NPAIR * LD)
        wvT = carve(NPAIR * LD)
        wout_in = carve(NPAIR * D).rearrange("p (j n) -> p j n", j=NPAIR)
        ZR = 2
        zero_rows = carve(ZR * D)
        attn.close()

        tail = ExitStack()
        ex_x = sb("ex_x", [P, 4, NB, D], F32, tail)
        ex_w = sb("ex_w", [P, 4, 3, 2, D], F32, tail)
        ex_xT = sb("ex_xT", [P, 4, KD, C], F32, tail)
        ex_s = sb("ex_s", [P, 4, KF, C], F32, tail)
        ex_h = sb("ex_h", [P, 4, KF, C], F32, tail)
        ex_y = sb("ex_y", [P, 4, NB, D], F32, tail)
        NL = 4
        LAST = B * NT // (2 * NL)
        last_y = sb("last_y", [P, 2 * NL, D], F32, tail)
        last_idx = sb("last_idx", [P, 2 * NL], I32, tail)
        last_o = sb("last_o", [P, 2 * NL, D], F32, tail)
        tail.close()

        const_ready = sem("const_ready")
        w_loaded = sem("w_loaded")
        zeroed = sem("zeroed")
        ring_full = sem("ring_full")
        ring_free = [sem(f"ring_free{i}") for i in range(2)]
        x_loaded = sem("x_loaded")
        xres_loaded = sem("xres_loaded")
        lat_hi_done = sem("lat_hi_done")
        lat_full = sem("lat_full")
        lat_ready = sem("lat_ready")
        fold_staged = sem("fold_staged")
        q_hi_done = sem("q_hi_done")
        score_full = sem("score_full")
        max_done = sem("max_done")
        exp_done = sem("exp_done")
        pv_done = sem("pv_done")
        head_done = sem("head_done")
        dve_step = sem("dve_step")
        var_ready = sem("var_ready")
        rstd_ready = sem("rstd_ready")
        x1_ready = sem("x1_ready")
        x1_kept = sem("x1_kept")
        logit_full = sem("logit_full")
        logit_ready = sem("logit_ready")
        gate_exp = sem("gate_exp")
        onehot_ready = sem("onehot_ready")
        pos_full = sem("pos_full")
        pos_used = sem("pos_used")
        send_ready = sem("send_ready")
        sent = sem("sent")
        ex_loaded = [sem(f"ex_loaded{i}") for i in range(4)]
        ex_t_full = sem("ex_t_full")
        ex_t_ready = sem("ex_t_ready")
        ex_g_full = sem("ex_g_full")
        ex_s_ready = sem("ex_s_ready")
        ex_h_ready = [sem(f"ex_h_ready{f}") for f in range(KF)]
        ex_y_full = sem("ex_y_full")
        ex_y_free = [sem(f"ex_y_free{i}") for i in range(2)]
        ex_stored = [sem(f"ex_stored{i}") for i in range(4)]
        idx_ready = sem("idx_ready")
        fetched = [sem(f"fetched{i}") for i in range(2)]
        last_ready = [sem(f"last_ready{i}") for i in range(2)]
        out_stored = [sem(f"out_stored{i}") for i in range(2)]

        PRIMED = 1
        primed = [head_done, pos_used, x1_kept, ex_t_ready, *ex_h_ready, *ex_y_free, *ex_stored,
                  *last_ready, *out_stored]

        def numbered(uses):
            assert len(uses) % 2 == 0
            return {u: i for i, u in enumerate(uses)}

        STEPS = [(0, i) for i in range(NT)] + [(1, i) for i in reversed(range(NT))]
        NS = len(STEPS)
        chunks = lambda i: [(c, min(HPB, i + 1 - HPB * c)) for c in range((i + HPB) // HPB)]
        probT_uses = lambda s: [("probT", s, c) for c, _ in chunks(STEPS[s][1])]
        SETUP = numbered([("wqT", c) for c in range(4)] + [("wkT", 0), ("wvT", 0)]
                         + [("A", h, kd) for h in range(2) for kd in range(KD)]
                         + [("V", h, c) for h in range(2) for c in range(4)])
        START = numbered([("xT", c) for c in range(4)] + [("lat", 0), ("lat", 1)] + [("q", 0), ("q", 1)])
        pair_uses = []
        for s in range(NS):
            pair_uses += probT_uses(s)
            if s == 1:
                pair_uses += [("headsT", 0), ("headsT", 1)]
            if s == NS - 3:
                pair_uses += [("q", 0), ("q", 1)]
        PAIR = numbered(pair_uses)
        END = numbered([("headsT", 0), ("headsT", 1)] + [("proj", i) for i in range(NT)]
                       + [("x1T", c) for c in range(4)])
        BATCH_USES = len(START) + NPAIR * len(PAIR) + len(END)

        def ring_halves(b):
            start = len(SETUP) // 2 + b * (BATCH_USES // 2)
            return start, start + len(START) // 2, start + (len(START) + NPAIR * len(PAIR)) // 2

        def ring_bases(b):
            start = len(SETUP) + b * BATCH_USES
            return start, start + len(START), start + len(START) + NPAIR * len(PAIR)

        PAIR_STEPS = 2
        END_STEPS = NT + 1 + 7 + (NT - 1) + 9

        def y_use(u, n):
            return (u * NB + n) % 2, (u * NB + n) // 2

        def chunk_engine(i, c):
            return "act" if (c == 1 or i in (2, 3)) else "dve"

        block = ctx.enter_context(nc.Block())

        def wait_alone(eng, sem, value):
            eng.compute_val(value)
            eng.wait_ge(const_ready, 15)
            eng.wait_ge(sem, value)

        @block.sync
        def _(sp):
            for s in primed:
                sp.sem_inc(s, PRIMED)
            sp.dma_start(wq_in, Wq.rearrange("(k p) h e -> p k (h e)", p=P)).then_inc(w_loaded, 16)
            sp.dma_start(wk_in[0:LD, :], Wk_up.rearrange("c h e -> c (h e)")).then_inc(w_loaded, 16)
            sp.dma_start(wv_in[0:LD, :], Wv_up.rearrange("c h e -> c (h e)")).then_inc(w_loaded, 16)
            sp.dma_start(wout_in, Wout.rearrange("(j h) e o -> (h e) j o", h=2)).then_inc(w_loaded, 16)
            sp.dma_start(wkv2[:, :, 0, :], Wkv.rearrange("(k p) c -> p k c", p=P)).then_inc(w_loaded, 16)
            sp.dma_start(wkv2[:, :, 1, :], Wkv.rearrange("(k p) c -> p k c", p=P)).then_inc(w_loaded, 16)
            sp.dma_start(wr[:, :, :], w_router.rearrange("(k p) e -> p k e", p=P)).then_inc(w_loaded, 16)
            sp.wait_ge(const_ready, 1)
            zero_view = slots_x.rearrange("(n r p) d -> n p r d", r=ZR, p=P)
            for n in range(zero_view.shape[0]):
                sp.dma_start(zero_view[n], zero_rows.rearrange("p (r d) -> p r d", r=ZR)).then_inc(zeroed, 16)
            sp.dma_start(x_in[:, :, :], x_tiles[0]).then_inc(x_loaded, 16)
            sp.dma_start(x_res[:, :, :], x_tiles[0]).then_inc(xres_loaded, 16)
            with sp.Fori(0, B - 1) as b:
                sp.wait_ge(ring_full, ring_bases(b)[1])
                sp.dma_start(x_in[:, :, :], x_tiles[bass.ds(b + 1, 1)].rearrange("b p t d -> p (b t) d")
                             ).then_inc(x_loaded, 16)
                sp.wait_ge(x1_ready, b + 1)
                sp.dma_start(x_res[:, :, :], x_tiles[bass.ds(b + 1, 1)].rearrange("b p t d -> p (b t) d")
                             ).then_inc(xres_loaded, 16)
            sp.wait_ge(x1_kept, B + PRIMED)

            def load_experts(g, sub):
                for u in range(2):
                    e, k = g * 4 + (sub * 2 + u), sub * 2 + u
                    for m, w in enumerate((w_gate, w_up, w_down)):
                        sp.dma_start(ex_w[:, k, m], w[bass.ds(e, 1)].rearrange("e (k p) f -> p (e k) f", p=P)
                                     ).then_inc(ex_loaded[k], 16)
                    rows = slots_x.rearrange("(e c) d -> e c d", c=C)[bass.ds(e, 1)]
                    for n, (r0, nr) in enumerate(BLOCKS):
                        sp.dma_start(ex_x[0:nr, k, n, :], rows[:, r0:r0 + nr, :].rearrange("e p d -> p (e d)")
                                     ).then_inc(ex_loaded[k], 16)

            load_experts(0, 0)
            with sp.Fori(0, E // 4 - 1) as g:
                for i in range(2):
                    sp.wait_ge(ex_y_free[i], g * (2 * NB) + PRIMED)
                load_experts(g, 1)
                for i in range(2):
                    sp.wait_ge(ex_y_free[i], g * (2 * NB) + NB + PRIMED)
                load_experts(g + 1, 0)
            for i in range(2):
                sp.wait_ge(ex_y_free[i], (E // 4 - 1) * 2 * NB + PRIMED)
            load_experts(E // 4 - 1, 1)
            with sp.Fori(0, LAST) as g:
                for u in range(2):
                    sp.wait_ge(last_ready[u], g + 1 + PRIMED)
                    sp.dma_start(out_tiles[bass.ds((g * 2 + u) * NL, NL)].rearrange("t p d -> p t d"),
                                 last_o[:, u * NL:(u + 1) * NL, :]).then_inc(out_stored[u], 16)
            for u in range(2):
                sp.wait_ge(out_stored[u], 16 * LAST + PRIMED)

        @block.gpsimd
        def _(pool):
            nc.gpsimd.memset(zero_rows, 0.0).then_inc(const_ready, 1)
            nc.gpsimd.memset(fold_q[:, :, NPAIR * P:], 0.0).then_inc(const_ready, 1)
            nc.gpsimd.memset(heads[:, :, :], 0.0).then_inc(const_ready, 1)
            nc.gpsimd.memset(earlier[:, :, :], 0.0).then_inc(const_ready, 1)
            nc.gpsimd.memset(ident[:, :], 0.0).then_inc(const_ready, 1)
            nc.gpsimd.memset(future_bf[:, :], 0.0).then_inc(const_ready, 1)
            nc.gpsimd.memset(before_bf[:, :], 1.0).then_inc(const_ready, 1)
            nc.gpsimd.memset(ones_bf[:, :], 1.0).then_inc(const_ready, 1)
            nc.gpsimd.memset(minus_half[:, :], -0.5).then_inc(const_ready, 1)
            nc.gpsimd.iota(expert_i[:, :], [[1, E]], base=-E, channel_multiplier=0).then_inc(const_ready, 1)
            pool.wait_ge(const_ready, 10)
            nc.gpsimd.affine_select(out=ident[:, :], in_=ident[:, :], pattern=[[-1, P]], compare_op=ALU.not_equal,
                                    fill=1.0, base=0, channel_multiplier=1).then_inc(const_ready, 1)
            nc.gpsimd.affine_select(out=future_bf[:, :], in_=future_bf[:, :], pattern=[[-1, P]], compare_op=ALU.is_ge,
                                    fill=MASKED, base=0, channel_multiplier=1).then_inc(const_ready, 1)
            nc.gpsimd.affine_select(out=before_bf[:, :], in_=before_bf[:, :], pattern=[[1, P]], compare_op=ALU.is_gt,
                                    fill=0.0, base=0, channel_multiplier=-1).then_inc(const_ready, 1)
            nc.gpsimd.tensor_copy(expert_m[:, :], expert_i[:, :]).then_inc(const_ready, 1)
            pool.wait_ge(const_ready, 14)
            nc.gpsimd.tensor_copy(ident_bf[:, :], ident[:, :]).then_inc(const_ready, 1)
            for k in range(2):
                pool.wait_ge(ring_free[k], len(SETUP) // 2)
            nc.gpsimd.tensor_copy(fold_stage[:, :, :], fold_q[:, :, 0:P]).then_inc(fold_staged, 1)
            with pool.Fori(0, B) as b:
                pairs = ring_bases(b)[1]
                with pool.Fori(0, NPAIR) as p:
                    wait_alone(pool, ring_full, pairs + p * len(PAIR))
                    nc.gpsimd.tensor_copy(fold_stage[:, :, :], fold_q[:, :, bass.ds((p + 1) * P, P)]
                                          ).then_inc(fold_staged, 1)
                wait_alone(pool, var_ready, b + 1)
                nc.gpsimd.tensor_tensor(rstd[:, :], var_eps[:, :], minus_half[:, :], ALU.pow).then_inc(rstd_ready, 1)
                pool.wait_ge(zeroed, 16 * (SLOTS // (ZR * P)))
                wait_alone(pool, send_ready, b + 1)
                for i in range(NT):
                    nc.gpsimd.indirect_dma_start(
                        out=slots_x, out_offset=bass.IndirectOffsetOnAxis(ap=send_idx[:, i:i + 1], axis=0),
                        in_=x1[:, i, :], in_offset=None, bounds_check=SLOTS - 1, oob_is_err=False).then_inc(sent, 16)
                wait_alone(pool, ring_full, ring_bases(b)[0] + BATCH_USES)
                nc.gpsimd.tensor_copy(fold_stage[:, :, :], fold_q[:, :, 0:P]).then_inc(fold_staged, 1)
                wait_alone(pool, sent, (b + 1) * (16 * NT))
                nc.gpsimd.tensor_copy(x1_all[:, bass.ds(b * NT, NT), :], x1[:, :, :]).then_inc(x1_kept, 1)
            for k in range(4):
                pool.wait_ge(ex_stored[k], 16 * NB * (E // 4) + PRIMED)
            def fetch(n, u):
                nc.gpsimd.tensor_copy(last_idx[:, u * NL:(u + 1) * NL], fetch_all[:, bass.ds(n * NL, NL)]
                                      ).then_inc(idx_ready, 1)
                wait_alone(pool, idx_ready, n + 1)
                for i in range(NL):
                    nc.gpsimd.indirect_dma_start(
                        out=last_y[:, u * NL + i, :], out_offset=None, in_=slots_y,
                        in_offset=bass.IndirectOffsetOnAxis(ap=last_idx[:, u * NL + i:u * NL + i + 1], axis=0),
                        bounds_check=SLOTS - 1, oob_is_err=False).then_inc(fetched[u], 16)

            def root(n, u):
                half_ = slice(u * NL, (u + 1) * NL)
                wait_alone(pool, var_ready, n + (B + 1))
                nc.gpsimd.tensor_tensor(rstd[:, half_], var_eps[:, half_], minus_half[:, half_], ALU.pow
                                        ).then_inc(rstd_ready, 1)

            fetch(0, 0)
            with pool.Fori(0, LAST - 1) as g:
                wait_alone(pool, last_ready[1], g + PRIMED)
                fetch(g * 2 + 1, 1)
                root(g * 2, 0)
                wait_alone(pool, last_ready[0], g + 1 + PRIMED)
                fetch(g * 2 + 2, 0)
                root(g * 2 + 1, 1)
            wait_alone(pool, last_ready[1], LAST - 1 + PRIMED)
            fetch(LAST * 2 - 1, 1)
            root(LAST * 2 - 2, 0)
            root(LAST * 2 - 1, 1)

        @block.tensor
        def _(pe):
            half = {"setup": 0}

            def ring_wait(part, uses, use):
                n = uses[use]
                pe.wait_ge(ring_free[n % 2], half[part] + n // 2)
                return ring[n % 2]

            def evacuated(part, uses, use):
                n = uses[use]
                pe.wait_ge(ring_free[n % 2], half[part] + n // 2 + 1)

            pe.wait_ge(const_ready, 15)
            pe.wait_ge(w_loaded, 16 * 7)
            for c in range(4):
                bank = ring_wait("setup", SETUP, ("wqT", c))
                for k in range(4):
                    j, kd = 2 * c + k // 2, k % 2
                    mm = nc.tensor.transpose(bank[:, k * P:(k + 1) * P], wq_in[:, kd, j * P:(j + 1) * P], ident[:, :])
                mm.then_inc(ring_full, 1)
            for name, w in (("wkT", wk_in), ("wvT", wv_in)):
                bank = ring_wait("setup", SETUP, (name, 0))
                for j in range(NPAIR):
                    mm = nc.tensor.transpose(bank[:, j * LD:(j + 1) * LD], w[0:LD, j * P:(j + 1) * P], ident[0:LD, 0:LD])
                mm.then_inc(ring_full, 1)
            for c in range(4):
                evacuated("setup", SETUP, ("wqT", c))
            evacuated("setup", SETUP, ("wkT", 0))
            evacuated("setup", SETUP, ("wvT", 0))
            for h in range(2):
                rows = slice(h * HD, (h + 1) * HD)
                for kd in range(KD):
                    bank = ring_wait("setup", SETUP, ("A", h, kd))
                    for j in range(NPAIR):
                        mm = nc.tensor.matmul(bank[:, j * LD:(j + 1) * LD],
                                              wqT[rows, j * D + kd * P:j * D + (kd + 1) * P],
                                              wkT[rows, j * LD:(j + 1) * LD], start=True, stop=True)
                    mm.then_inc(ring_full, 1)
            for h in range(2):
                rows = slice(h * HD, (h + 1) * HD)
                for c in range(4):
                    bank = ring_wait("setup", SETUP, ("V", h, c))
                    for j in (2 * c, 2 * c + 1):
                        mm = nc.tensor.matmul(bank[rows, (j % 2) * D:(j % 2 + 1) * D], wvT[rows, j * LD:(j + 1) * LD],
                                              wout_in[rows, j, :], start=True, stop=True)
                    mm.then_inc(ring_full, 1)
            for c in range(4):
                evacuated("setup", SETUP, ("V", 1, c))

            def project_q(base, uses, hf):
                bank = ring_wait(base, uses, ("q", hf))
                for kd in range(KD):
                    mm = nc.tensor.matmul(bank[:, :], fold_stage[:, kd, :], xT[:, kd, hf * BANK:(hf + 1) * BANK],
                                          start=(kd == 0), stop=(kd == KD - 1))
                mm.then_inc(ring_full, 1)

            def transpose_heads(base, uses):
                for c in range(2):
                    bank = ring_wait(base, uses, ("headsT", c))
                    for k in range(HPB):
                        mm = nc.tensor.transpose(bank[:, k * P:(k + 1) * P], heads[:, HPB * c + k, :], ident[:, :])
                    mm.then_inc(ring_full, 1)

            with pe.Fori(0, B) as b:
                half["start"] = pe.snap(ring_halves(b)[0])
                pe.wait_ge(x_loaded, (b + 1) * 16)
                for c in range(4):
                    bank = ring_wait("start", START, ("xT", c))
                    kd, t0 = c // 2, HPB * (c % 2)
                    for k in range(HPB):
                        mm = nc.tensor.transpose(bank[:, k * P:(k + 1) * P], x_in[:, t0 + k, kd * P:(kd + 1) * P],
                                                 ident[:, :])
                    mm.then_inc(ring_full, 1)
                for hf in range(2):
                    evacuated("start", START, ("xT", hf))
                    evacuated("start", START, ("xT", 2 + hf))
                    bank = ring_wait("start", START, ("lat", hf))
                    for kd in range(KD):
                        mm = nc.tensor.matmul(bank[:, :], wkv2[:, kd].rearrange("p a c -> p (a c)"),
                                              xT[:, kd, hf * BANK:(hf + 1) * BANK], start=(kd == 0), stop=(kd == KD - 1))
                    mm.then_inc(ring_full, 1)
                pe.wait_ge(fold_staged, b * (NPAIR + 1) + 1)
                for hf in range(2):
                    project_q("start", START, hf)
                pe.wait_ge(pos_used, b + PRIMED)
                for i in range(NT):
                    for kd in range(KD):
                        mm = nc.tensor.matmul(head_ps[0][:, i * LD:(i + 1) * LD], xT[:, kd, i * P:(i + 1) * P],
                                              wkv2[:, kd, 0, :], start=(kd == 0), stop=(kd == KD - 1))
                mm.then_inc(lat_full, 1)
                pe.wait_ge(lat_ready, b + 1)
                wait_alone(pe, ring_free[0], half["start"] + len(START) // 2)
                pe.wait_ge(ring_free[1], half["start"] + len(START) // 2)

                with pe.Fori(0, NPAIR) as p:
                    half["pair"] = pe.snap(ring_halves(b)[1] + p * (len(PAIR) // 2))
                    pair = b * NPAIR + p
                    tile0 = pe.snap(pair * NS)

                    def scores(s):
                        h, i = STEPS[s]
                        if s >= 2:
                            pe.wait_ge(exp_done, tile0 + s - 1)
                        keys = (i + 1) * P
                        for k0 in range(0, keys, BANK):
                            k1 = min(keys, k0 + BANK)
                            dst = score_ps[s % 2]
                            q = q_hl[:, h, i * P:(i + 1) * P]
                            nc.tensor.matmul(dst[:, k0:k1], q, lat_hi[:, k0:k1], start=True, stop=False)
                            if k1 == keys:
                                nc.tensor.matmul(dst[:, keys - P:keys], ident_bf[:, :], future_bf[:, :],
                                                 start=False, stop=False)
                            mm = nc.tensor.matmul(dst[:, k0:k1], q, lat_lo[:, k0:k1], start=False, stop=True)
                        mm.then_inc(score_full, 1)

                    def transpose_probs(s):
                        h, i = STEPS[s]
                        pe.wait_ge(exp_done, tile0 + s + 1)
                        for c, n in chunks(i):
                            bank = ring_wait("pair", PAIR, ("probT", s, c))
                            for k in range(n):
                                j = HPB * c + k
                                mm = nc.tensor.transpose(bank[:, k * P:(k + 1) * P], probs[:, s % 2, j * P:(j + 1) * P],
                                                         ident[:, :])
                            mm.then_inc(ring_full, 1)

                    def times_latents(s):
                        h, i = STEPS[s]
                        for c, n in chunks(i):
                            evacuated("pair", PAIR, ("probT", s, c))
                            for k in range(n):
                                j = HPB * c + k
                                mm = nc.tensor.matmul(head_ps[h][:, i * LD:(i + 1) * LD],
                                                      probsT[:, s % 2, j * P:(j + 1) * P], lat[:, j, :],
                                                      start=(j == 0), stop=(j == i))
                        mm.then_inc(pv_done, 1)

                    scores(0)
                    scores(1)
                    for s in range(NS):
                        if s + 2 < NS:
                            scores(s + 2)
                        transpose_probs(s)
                        if s == 1:
                            pe.wait_ge(head_done, pair * 2 + PRIMED)
                            transpose_heads("pair", PAIR)
                        if s == NS - 3:
                            pe.wait_ge(fold_staged, b * (NPAIR + 1) + p + 2)
                            for hf in range(2):
                                project_q("pair", PAIR, hf)
                        if s >= 1:
                            times_latents(s - 1)
                    times_latents(NS - 1)

                half["end"] = pe.snap(ring_halves(b)[2])
                pe.wait_ge(head_done, (b + 1) * NPAIR * 2 + PRIMED)
                transpose_heads("end", END)
                for c in range(2):
                    evacuated("end", END, ("headsT", c))
                for i in range(NT):
                    bank = ring_wait("end", END, ("proj", i))
                    for j in range(NPAIR):
                        mm = nc.tensor.matmul(bank[:, 0:D], headsT[:, j + 1, i * P:(i + 1) * P], fold_v[:, j, :],
                                              start=(j == 0), stop=(j == NPAIR - 1))
                    mm.then_inc(ring_full, 1)
                pe.wait_ge(x1_ready, b + 1)
                for c in range(4):
                    bank = ring_wait("end", END, ("x1T", c))
                    kd, t0 = c // 2, HPB * (c % 2)
                    for k in range(HPB):
                        mm = nc.tensor.transpose(bank[:, k * P:(k + 1) * P], x1[:, t0 + k, kd * P:(kd + 1) * P],
                                                 ident[:, :])
                    mm.then_inc(ring_full, 1)
                for c in range(4):
                    evacuated("end", END, ("x1T", c))
                for i in range(NT):
                    for kd in range(KD):
                        mm = nc.tensor.matmul(head_ps[0][:, i * E:(i + 1) * E], xT[:, kd, i * P:(i + 1) * P],
                                              wr[:, kd, :], start=(kd == 0), stop=(kd == KD - 1))
                mm.then_inc(logit_full, 1)
                pe.wait_ge(onehot_ready, b + 1)
                nc.tensor.matmul(head_ps[1][:, 0:NT * E], before_bf[:, :], onehot[:, :, :].rearrange("p t e -> p (t e)"),
                                 start=True, stop=False)
                nc.tensor.matmul(head_ps[1][:, 0:NT * E], ones_bf[:, :],
                                 earlier[:, 0:NT, :].rearrange("p t e -> p (t e)"),
                                 start=False, stop=True).then_inc(pos_full, 1)

            pe.wait_ge(pos_used, B + PRIMED)
            with pe.Fori(0, E // 4) as g:
                for sub in range(2):
                    for u in range(2):
                        k, e = sub * 2 + u, g * 4 + (sub * 2 + u)
                        pe.wait_ge(ex_loaded[k], (g + 1) * (16 * (3 + NB)))
                        pe.wait_ge(ex_t_ready, e + PRIMED)
                        for kd in range(KD):
                            for n, (r0, nr) in enumerate(BLOCKS):
                                mm = nc.tensor.transpose(ring[kd][:, r0:r0 + nr], ex_x[0:nr, k, n, kd * P:(kd + 1) * P],
                                                         ident[0:nr, 0:nr])
                        mm.then_inc(ex_t_full, 1)
                    for u in range(2):
                        k, e = sub * 2 + u, g * 4 + (sub * 2 + u)
                        pe.wait_ge(ex_t_ready, e + 1 + PRIMED)
                        for f in range(KF):
                            pe.wait_ge(ex_h_ready[f], e + PRIMED)
                            for m in range(2):
                                for kd in range(KD):
                                    mm = nc.tensor.matmul(score_ps[f][:, m * BANK:m * BANK + C],
                                                          ex_w[:, k, m, kd, f * P:(f + 1) * P], ex_xT[:, k, kd, :],
                                                          start=(kd == 0), stop=(kd == KD - 1))
                            mm.then_inc(ex_g_full, 1)
                    for u in range(2):
                        k, e = sub * 2 + u, g * 4 + (sub * 2 + u)
                        for f in range(KF):
                            pe.wait_ge(ex_h_ready[f], e + 1 + PRIMED)
                        for n, (r0, nr) in enumerate(BLOCKS):
                            bank, uses = y_use(u, n)
                            pe.wait_ge(ex_y_free[bank], g * (2 * NB) + (sub * NB + uses) + PRIMED)
                            for f in range(KF):
                                mm = nc.tensor.matmul(head_ps[bank][0:nr, 0:D], ex_h[:, k, f, r0:r0 + nr],
                                                      ex_w[:, k, 2, f, :], start=(f == 0), stop=(f == KF - 1))
                            mm.then_inc(ex_y_full, 1)

        @block.scalar
        def _(act):
            def full(base, uses, use):
                n = uses[use]
                act.wait_ge(ring_full, base + n + 1)
                return ring[n % 2], ring_free[n % 2]

            for name, dst in (("wkT", wkT), ("wvT", wvT)):
                bank, done = full(0, SETUP, (name, 0))
                nc.scalar.copy(dst, bank[:, :]).then_inc(done, 1)
            for h in range(2):
                rows = slice(h * HD, (h + 1) * HD)
                for c in range(4):
                    bank, done = full(0, SETUP, ("V", h, c))
                    nc.scalar.copy(fold_v[rows, 2 * c:2 * c + 2, :].rearrange("p j n -> p (j n)"), bank[rows, :]
                                   ).then_inc(done, 1)

            def split_hi(base, uses, hf):
                bank, _ = full(base, uses, ("q", hf))
                cols = slice(hf * BANK, (hf + 1) * BANK)
                nc.scalar.copy(q_hl[0:64, 0, cols], bank[0:64, :])
                nc.scalar.copy(q_hl[64:128, 1, cols], bank[64:128, :]).then_inc(q_hi_done, 1)

            with act.Fori(0, B) as b:
                start, pairs, end = ring_bases(b)
                start = act.snap(start)
                for c in (1, 3):
                    bank, done = full(start, START, ("xT", c))
                    nc.scalar.copy(xT[:, c // 2, (c % 2) * BANK:(c % 2 + 1) * BANK], bank[:, :]).then_inc(done, 1)
                for hf in range(2):
                    bank, _ = full(start, START, ("lat", hf))
                    nc.scalar.copy(lat_hi[:, hf * BANK:(hf + 1) * BANK], bank[:, :]).then_inc(lat_hi_done, 1)
                for hf in range(2):
                    split_hi(start, START, hf)
                act.wait_ge(lat_full, b + 1)
                nc.scalar.copy(lat[:, :, :].rearrange("p t c -> p (t c)"), head_ps[0][:, :]).then_inc(lat_ready, 1)

                with act.Fori(0, NPAIR) as p:
                    base = act.snap(pairs + p * len(PAIR))
                    tile0 = act.snap((b * NPAIR + p) * NS)

                    def evacuate_probs(s):
                        h, i = STEPS[s]
                        for c, n in chunks(i):
                            if chunk_engine(i, c) == "act":
                                if s >= 2:
                                    act.wait_ge(pv_done, tile0 + s - 1)
                                bank, done = full(base, PAIR, ("probT", s, c))
                                nc.scalar.copy(probsT[:, s % 2, c * BANK:c * BANK + n * P], bank[:, 0:n * P]
                                               ).then_inc(done, 1)

                    act.wait_ge(head_done, (b * NPAIR + p) * 2 + PRIMED)
                    for s in range(NS):
                        h, i = STEPS[s]
                        keys = (i + 1) * P
                        act.wait_ge(max_done, tile0 + s + 1)
                        if s >= 2:
                            act.wait_ge(ring_full, base + PAIR[probT_uses(s - 2)[-1]] + 1)
                        nc.scalar.activation(probs[:, s % 2, 0:keys], score_ps[s % 2][:, 0:keys], ACT.Exp,
                                             bias=negmax[:, h * NT + i:h * NT + i + 1],
                                             accum_out=rowsum[:, h * NT + i:h * NT + i + 1]).then_inc(exp_done, 1)
                        if s >= 1:
                            evacuate_probs(s - 1)
                        if s == 2:
                            for c in range(2):
                                bank, done = full(base, PAIR, ("headsT", c))
                                nc.scalar.copy(headsT[:, bass.ds(p, 1), c * BANK:(c + 1) * BANK].rearrange("p a n -> p (a n)"),
                                               bank[:, :]).then_inc(done, 1)
                        if s == NS - 2:
                            for hf in range(2):
                                split_hi(base, PAIR, hf)
                    evacuate_probs(NS - 1)

                end = act.snap(end)
                for c in range(2):
                    bank, done = full(end, END, ("headsT", c))
                    nc.scalar.copy(headsT[:, NPAIR, c * BANK:(c + 1) * BANK], bank[:, :]).then_inc(done, 1)
                for c in (1, 3):
                    bank, done = full(end, END, ("x1T", c))
                    nc.scalar.copy(xT[:, c // 2, (c % 2) * BANK:(c % 2 + 1) * BANK], bank[:, :]).then_inc(done, 1)
                act.wait_ge(logit_ready, b + 1)
                nc.scalar.activation(work_b[:, :, :], work_a[:, :, :], ACT.Exp).then_inc(gate_exp, 1)

            with act.Fori(0, E // 4) as g:
                for sub in range(2):
                    for u in range(2):
                        k, e = sub * 2 + u, g * 4 + (sub * 2 + u)
                        act.wait_ge(ex_t_full, e + 1)
                        nc.scalar.copy(ex_xT[:, k, 0, :], ring[0][:, 0:C])
                        nc.scalar.copy(ex_xT[:, k, 1, :], ring[1][:, 0:C]).then_inc(ex_t_ready, 1)
                    for u in range(2):
                        k, e = sub * 2 + u, g * 4 + (sub * 2 + u)
                        for f in range(KF):
                            act.wait_ge(ex_g_full, e * KF + (f + 1))
                            nc.scalar.activation(ex_s[:, k, f, :], score_ps[f][:, 0:C], ACT.Silu).then_inc(ex_s_ready, 1)
                    for u in range(2):
                        k, e = sub * 2 + u, g * 4 + (sub * 2 + u)
                        for n in range(max(0, NB - 2), NB):
                            bank, uses = y_use(u, n)
                            act.wait_ge(ex_y_free[bank], g * (2 * NB) + (sub * NB + uses + 1) + PRIMED)
                        rows = slots_y.rearrange("(e c) d -> e c d", c=C)[bass.ds(e, 1)]
                        for n, (r0, nr) in enumerate(BLOCKS):
                            act.dma_start(rows[:, r0:r0 + nr, :].rearrange("e p d -> p (e d)"), ex_y[0:nr, k, n, :]
                                          ).then_inc(ex_stored[k], 16)

        @block.vector
        def _(dve):
            def full(base, uses, use):
                n = uses[use]
                dve.wait_ge(ring_full, base + n + 1)
                return ring[n % 2], ring_free[n % 2]

            steps = [0, 0]

            def step(ins):
                steps[1] += 1
                ins.then_inc(dve_step, 1)

            def settle(alone=False):
                if alone:
                    wait_alone(dve, dve_step, steps[0] + steps[1])
                else:
                    dve.wait_ge(dve_step, steps[0] + steps[1])

            for c in range(4):
                bank, done = full(0, SETUP, ("wqT", c))
                nc.vector.tensor_copy(wqT[:, c * BANK:(c + 1) * BANK], bank[:, :]).then_inc(done, 1)
            for h in range(2):
                for kd in range(KD):
                    bank, done = full(0, SETUP, ("A", h, kd))
                    dst = fold_q[:, kd, 0:NPAIR * P].rearrange("p (j h c) -> p j h c", h=2, c=LD)[:, :, h, :]
                    nc.vector.tensor_scalar(dst, bank[:, :].rearrange("p (j c) -> p j c", c=LD),
                                            float(HD) ** -0.5, None, ALU.mult).then_inc(done, 1)

            def split_lo(base, uses, hf, count):
                dve.wait_ge(q_hi_done, count + hf + 1)
                bank, done = full(base, uses, ("q", hf))
                cols = slice(hf * BANK, (hf + 1) * BANK)
                nc.vector.tensor_tensor(q_hl[64:128, 0, cols], bank[0:64, :], q_hl[0:64, 0, cols].bitcast(F32),
                                        ALU.subtract)
                nc.vector.tensor_tensor(q_hl[0:64, 1, cols], bank[64:128, :], q_hl[64:128, 1, cols].bitcast(F32),
                                        ALU.subtract).then_inc(done, 1)

            with dve.Fori(0, B) as b:
                start, pairs, end = ring_bases(b)
                start = dve.snap(start)
                for c in (0, 2):
                    bank, done = full(start, START, ("xT", c))
                    nc.vector.tensor_copy(xT[:, c // 2, (c % 2) * BANK:(c % 2 + 1) * BANK], bank[:, :]).then_inc(done, 1)
                for hf in range(2):
                    dve.wait_ge(lat_hi_done, b * 2 + hf + 1)
                    bank, done = full(start, START, ("lat", hf))
                    cols = slice(hf * BANK, (hf + 1) * BANK)
                    nc.vector.tensor_tensor(lat_lo[:, cols], bank[:, :], lat_hi[:, cols].bitcast(F32), ALU.subtract
                                            ).then_inc(done, 1)
                for hf in range(2):
                    split_lo(start, START, hf, b * ((NPAIR + 1) * 2))

                with dve.Fori(0, NPAIR) as p:
                    base = dve.snap(pairs + p * len(PAIR))
                    tile0 = dve.snap((b * NPAIR + p) * NS)
                    steps[0] = dve.snap(b * (NPAIR * PAIR_STEPS + END_STEPS) + p * PAIR_STEPS)
                    steps[1] = 0

                    def evacuate_probs(s):
                        h, i = STEPS[s]
                        for c, n in chunks(i):
                            if chunk_engine(i, c) == "dve":
                                if s >= 2:
                                    dve.wait_ge(pv_done, tile0 + s - 1)
                                bank, done = full(base, PAIR, ("probT", s, c))
                                nc.vector.tensor_copy(probsT[:, s % 2, c * BANK:c * BANK + n * P], bank[:, 0:n * P]
                                                      ).then_inc(done, 1)

                    def normalise(h):
                        dve.wait_ge(exp_done, tile0 + NT * (h + 1))
                        step(nc.vector.reciprocal(rinv[:, h * NT:(h + 1) * NT], rowsum[:, h * NT:(h + 1) * NT]))
                        settle()
                        dve.wait_ge(pv_done, tile0 + NT * (h + 1))
                        dve.wait_ge(ring_full, base + PAIR[("headsT", 1)] + 1)
                        nc.vector.tensor_tensor(
                            heads[:, :, h * LD:(h + 1) * LD], head_ps[h][:, :].rearrange("p (t c) -> p t c", c=LD),
                            rinv[:, h * NT:(h + 1) * NT].unsqueeze(2).to_broadcast([P, NT, LD]), ALU.mult
                        ).then_inc(head_done, 1)

                    for s in range(NS):
                        h, i = STEPS[s]
                        dve.wait_ge(score_full, tile0 + s + 1)
                        nc.vector.tensor_reduce(negmax[:, h * NT + i:h * NT + i + 1], score_ps[s % 2][:, 0:(i + 1) * P],
                                                AX.X, ALU.max, negate=True).then_inc(max_done, 1)
                        if s >= 1:
                            evacuate_probs(s - 1)
                        if s == NT + 1:
                            normalise(0)
                        if s == NS - 2:
                            for hf in range(2):
                                split_lo(base, PAIR, hf, (b * (NPAIR + 1) + p + 1) * 2)
                    evacuate_probs(NS - 1)
                    normalise(1)
                    assert steps[1] == PAIR_STEPS

                end = dve.snap(end)
                steps[0] = dve.snap(b * (NPAIR * PAIR_STEPS + END_STEPS) + NPAIR * PAIR_STEPS)
                steps[1] = 0
                dve.wait_ge(xres_loaded, (b + 1) * 16)
                dve.wait_ge(x1_kept, b + PRIMED)
                end_half = dve.snap(ring_halves(b)[2])

                def statistics(i):
                    dve.wait_ge(ring_free[END[("proj", i)] % 2], end_half + (END[("proj", i)] // 2 + 1))
                    step(nc.vector.bn_stats(stat6[:, i, :], x1[:, i, :]))

                for i in range(NT):
                    bank, done = full(end, END, ("proj", i))
                    nc.vector.tensor_tensor(x1[:, i, :], bank[:, 0:D], x_res[:, i, :], ALU.add).then_inc(done, 1)
                    if i >= 1:
                        statistics(i - 1)
                statistics(NT - 1)
                settle(alone=True)
                for i in range(NT):
                    last = nc.vector.bn_aggr(mean_var[:, i, :], stat6[:, i, :])
                step(last)
                settle()
                nc.vector.tensor_scalar(var_eps[:, :], mean_var[:, :, 1], EPS, None, ALU.add).then_inc(var_ready, 1)
                dve.wait_ge(rstd_ready, b + 1)
                for i in range(NT):
                    last = nc.vector.tensor_scalar(x1[:, i, :], x1[:, i, :], mean_var[:, i, 0:1], rstd[:, i:i + 1],
                                                   ALU.subtract, ALU.mult)
                last.then_inc(x1_ready, 1)
                for c in (0, 2):
                    bank, done = full(end, END, ("x1T", c))
                    nc.vector.tensor_copy(xT[:, c // 2, (c % 2) * BANK:(c % 2 + 1) * BANK], bank[:, :]).then_inc(done, 1)
                over = lambda k: rt[:, k, :].unsqueeze(2).to_broadcast([P, NT, E])
                each = expert_m[:, :].unsqueeze(1).to_broadcast([P, NT, E])
                dve.wait_ge(logit_full, b + 1)
                step(nc.vector.tensor_copy(logit[:, :, :].rearrange("p t e -> p (t e)"), head_ps[0][:, 0:NT * E]))
                settle()
                step(nc.vector.tensor_reduce(rt[:, 0, :], logit[:, :, :], AX.X, ALU.max))
                settle()
                nc.vector.tensor_tensor(work_a[:, :, :], logit[:, :, :], over(0), ALU.subtract).then_inc(logit_ready, 1)
                step(nc.vector.tensor_tensor(logit[:, :, :], logit[:, :, :], over(0), ALU.is_equal))
                settle()
                step(nc.vector.tensor_tensor(logit[:, :, :], logit[:, :, :], each, ALU.mult))
                settle()
                step(nc.vector.tensor_reduce(rt[:, 3, :], logit[:, :, :], AX.X, ALU.min))
                settle()
                step(nc.vector.tensor_tensor(onehot[:, :, :], each, over(3), ALU.is_equal))
                step(nc.vector.tensor_copy(earlier[:, 0, :], earlier[:, NT, :]))
                settle()
                for i in range(NT):
                    ins = nc.vector.tensor_tensor(earlier[:, i + 1, :], earlier[:, i, :], onehot[:, i, :], ALU.add)
                    if i < NT - 1:
                        step(ins)
                        settle()
                ins.then_inc(onehot_ready, 1)
                dve.wait_ge(gate_exp, b + 1)
                step(nc.vector.tensor_reduce(rt[:, 1, :], work_b[:, :, :], AX.X, ALU.add))
                settle()
                step(nc.vector.reciprocal(rt[:, 2, :], rt[:, 1, :]))
                dve.wait_ge(pos_full, b + 1)
                step(nc.vector.tensor_tensor(work_a[:, :, :], onehot[:, :, :],
                                             head_ps[1][:, 0:NT * E].rearrange("p (t e) -> p t e", e=E), ALU.mult))
                settle()
                step(nc.vector.tensor_reduce(rt[:, 4, :], work_a[:, :, :], AX.X, ALU.add))
                settle()
                step(nc.vector.scalar_tensor_tensor(rt[:, 5, :], rt[:, 3, :], float(C), rt[:, 4, :], ALU.mult, ALU.add))
                step(nc.vector.tensor_scalar(rt[:, 6, :], rt[:, 4, :], float(C), None, ALU.is_lt))
                step(nc.vector.tensor_scalar(rt[:, 7, :], rt[:, 4, :], float(C), FAR, ALU.is_ge, ALU.mult))
                settle()
                step(nc.vector.scalar_tensor_tensor(rt[:, 8, :], rt[:, 5, :], float(SLOTS), rt[:, 7, :], ALU.add, ALU.add))
                step(nc.vector.tensor_tensor(gate_all[:, bass.ds(b * NT, NT)], rt[:, 2, :], rt[:, 6, :], ALU.mult))
                settle()
                nc.vector.tensor_scalar(fetch_all[:, bass.ds(b * NT, NT)], rt[:, 8, :], float(SLOTS - 1), None, ALU.min
                                        ).then_inc(pos_used, 1)
                nc.vector.tensor_copy(send_idx[:, :], rt[:, 8, :]).then_inc(send_ready, 1)
                assert steps[1] == END_STEPS, steps

            with dve.Fori(0, E // 4) as g:
                for sub in range(2):
                    for u in range(2):
                        k, e = sub * 2 + u, g * 4 + (sub * 2 + u)
                        for f in range(KF):
                            dve.wait_ge(ex_s_ready, e * KF + (f + 1))
                            nc.vector.tensor_tensor(ex_h[:, k, f, :], ex_s[:, k, f, :], score_ps[f][:, BANK:BANK + C],
                                                    ALU.mult).then_inc(ex_h_ready[f], 1)
                    for u in range(2):
                        k, e = sub * 2 + u, g * 4 + (sub * 2 + u)
                        dve.wait_ge(ex_stored[k], g * (16 * NB) + PRIMED)
                        for n, (r0, nr) in enumerate(BLOCKS):
                            bank, _ = y_use(u, n)
                            dve.wait_ge(ex_y_full, e * NB + (n + 1))
                            nc.vector.tensor_copy(ex_y[0:nr, k, n, :], head_ps[bank][0:nr, 0:D]
                                                  ).then_inc(ex_y_free[bank], 1)

            with dve.Fori(0, LAST) as g:
                steps[0] = dve.snap(B * (NPAIR * PAIR_STEPS + END_STEPS) + g * (2 * 4))
                steps[1] = 0
                for u in range(2):
                    n = g * 2 + u
                    half_ = slice(u * NL, (u + 1) * NL)
                    dve.wait_ge(fetched[u], (g + 1) * (16 * NL))
                    step(nc.vector.tensor_tensor(last_y[:, half_, :], last_y[:, half_, :],
                                                 gate_all[:, bass.ds(n * NL, NL)].unsqueeze(2).to_broadcast([P, NL, D]),
                                                 ALU.mult))
                    settle()
                    step(nc.vector.scalar_tensor_tensor(last_y[:, half_, :], x1_all[:, bass.ds(n * NL, NL), :], 2.0,
                                                        last_y[:, half_, :], ALU.mult, ALU.add))
                    settle()
                    for i in range(NL):
                        last = nc.vector.bn_stats(stat6[:, u * NL + i, :], last_y[:, u * NL + i, :])
                    step(last)
                    settle(alone=True)
                    for i in range(NL):
                        last = nc.vector.bn_aggr(mean_var[:, u * NL + i, :], stat6[:, u * NL + i, :])
                    step(last)
                    settle()
                    nc.vector.tensor_scalar(var_eps[:, half_], mean_var[:, half_, 1], EPS, None, ALU.add
                                            ).then_inc(var_ready, 1)
                    dve.wait_ge(rstd_ready, n + (B + 1))
                    dve.wait_ge(out_stored[u], g * 16 + PRIMED)
                    for i in range(NL):
                        k = u * NL + i
                        last = nc.vector.tensor_scalar(last_o[:, k, :], last_y[:, k, :], mean_var[:, k, 0:1],
                                                       rstd[:, k:k + 1], ALU.subtract, ALU.mult)
                    last.then_inc(last_ready[u], 1)


_INS = ["L0_attn_x_bld", "L0_attn_Wq", "L0_attn_Wkv_down", "L0_attn_Wk_up", "L0_attn_Wv_up", "L0_attn_Wout",
        "L0_ffn_w_router", "L0_ffn_w_gate", "L0_ffn_w_up", "L0_ffn_w_down"]
_OUT = "layer_out"


def kernel(**inputs):
    import concourse.bacc as bacc
    from concourse.bass_utils import run_bass_kernel_spmd

    nc = bacc.Bacc("TRN2", target_bir_lowering=False, num_devices=1)
    arrays, aps = {}, []
    for name in _INS:
        a = np.ascontiguousarray(inputs[name])
        arrays["in_" + name] = a
        aps.append(nc.dram_tensor("in_" + name, a.shape, mybir.dt.from_np(a.dtype), kind="ExternalInput").ap())
    aps.append(nc.dram_tensor(_OUT, inputs["L0_attn_x_bld"].shape, F32, kind="ExternalOutput").ap())
    build_layer(nc, *aps)
    result = run_bass_kernel_spmd(nc, [arrays], core_ids=[0])
    return result.results[0][_OUT]
```

```python
import math
from contextlib import ExitStack

import numpy as np

import concourse.bass as bass
from concourse import mybir

ALU = mybir.AluOpType
ACT = mybir.ActivationFunctionType
AX = mybir.AxisListType
F32 = mybir.dt.float32
F32R = mybir.dt.float32r
BF16 = mybir.dt.bfloat16
I32 = mybir.dt.int32

P = 128
BANK = 512
EPS = 1e-5
MASKED = -1e30
FAR = 2.0 ** 22


def build_layer(nc, x, Wq, Wkv, Wk_up, Wv_up, Wout, w_router, w_gate, w_up, w_down, out):
    B, L, D = x.shape
    _, H, HD = Wq.shape
    LD = Wkv.shape[1]
    E, _, F = w_gate.shape
    T = B * L
    C = int(math.ceil(1.25 * T / E))
    NT = L // P
    NPAIR = H // 2
    KD = D // P
    KF = F // P
    HPB = BANK // P
    assert HD == 64 and LD == 64 and KD == 2 and KF == 2 and NT == 8 and D == 256 and C <= BANK
    SLOTS = E * C
    BLOCKS = [(r, min(P, C - r)) for r in range(0, C, P)]
    NB = len(BLOCKS)

    ORDER = [7, 6, 3, 2, 5, 4, 1, 0]
    STEPS = [(h, i) for h in range(4) for i in ORDER]
    NS = len(STEPS)
    G = NPAIR // 2
    TPQ = 2
    NQ = NT // TPQ
    QUARTER = TPQ * P
    HI_LAG, LO_LAG = 2, 3
    NRING = 4
    NPROBS = 4
    chunks = lambda i: [(c, min(HPB, i + 1 - HPB * c)) for c in range((i + HPB) // HPB)]

    slots_x = nc.dram_tensor("slots_x", [SLOTS, D], F32, kind="Internal").ap()
    x1_rows = nc.dram_tensor("x1_rows", [T, D], F32, kind="Internal").ap()
    slots_y = nc.dram_tensor("slots_y", [SLOTS, D], F32, kind="Internal").ap()
    x_tiles = x.rearrange("b (t p) d -> b p t d", p=P)
    x1_tiles = x1_rows.rearrange("(b t p) d -> b p t d", t=NT, p=P)
    out_tiles = out.rearrange("b (t p) d -> (b t) p d", p=P)

    with ExitStack() as ctx:
        def sb(name, shape, dt=F32, stack=ctx):
            return stack.enter_context(nc.sbuf_tensor(name, shape, dt))

        def sem(name):
            return ctx.enter_context(nc.semaphore(name))

        score_ps = [ctx.enter_context(nc.psum_tensor(f"score_ps{i}", [P, 2 * BANK], F32)) for i in range(2)]
        ring = [ctx.enter_context(nc.psum_tensor(f"ring{i}", [P, BANK], F32)) for i in range(NRING)]

        gate_all = sb("gate_all", [P, B * NT])
        fetch_all = sb("fetch_all", [P, B * NT], I32)
        ident = sb("ident", [P, P])
        stat6 = sb("stat6", [P, 8, 6])
        mean_var = sb("mean_var", [P, 8, 2])
        var_eps = sb("var_eps", [P, 8])
        rstd = sb("rstd", [P, 8])
        minus_half = sb("minus_half", [P, 8])

        attn = ExitStack()
        ident_bf = sb("ident_bf", [P, P], BF16, attn)
        future_bf = sb("future_bf", [P, P], BF16, attn)
        before_bf = sb("before_bf", [P, P], BF16, attn)
        ones_bf = sb("ones_bf", [P, P], BF16, attn)
        expert_m = sb("expert_m", [P, E], F32, attn)
        expert_i = sb("expert_i", [P, E], I32, attn)
        x_in = sb("x_in", [P, NT, D], F32, attn)
        x_res = sb("x_res", [P, NT, D], F32, attn)
        xT = sb("xT", [P, KD, L], F32, attn)
        lat_hi = sb("lat_hi", [P, L], F32R, attn)
        lat_lo = sb("lat_lo", [P, L], F32R, attn)
        lat_keys = sb("lat_keys", [P, NT, 2, LD], F32R, attn)
        fold_q = sb("fold_q", [P, KD, (NPAIR + 2) * P], F32, attn)
        fold_stage = sb("fold_stage", [P, KD, P], F32, attn)
        fold_v = sb("fold_v", [P, NPAIR, D], F32, attn)
        q_hl = sb("q_hl", [P, 2, 2, L], F32R, attn)
        probs = sb("probs", [P, NPROBS, L], F32, attn)
        x1T = probs[:, NPROBS - KD:NPROBS, :]
        probsT_hi = [sb(f"probsT_hi{c}", [P, TPQ * (c + 1), QUARTER], F32R, attn) for c in range(NQ)]
        probsT_lo = [sb(f"probsT_lo{c}", [P, TPQ * (c + 1), QUARTER], F32R, attn) for c in range(NQ)]
        negmax = sb("negmax", [P, NS], F32, attn)
        rowsum = sb("rowsum", [P, 4, NT], F32, attn)
        rinv = sb("rinv", [P, 4, NT], F32, attn)
        rinv_wide = sb("rinv_wide", [P, NT, 2, LD], F32, attn)
        rinv_rows = sb("rinv_rows", [P, L], F32, attn)
        low_sum = sb("low_sum", [P, NQ, QUARTER], F32, attn)
        headsT = sb("headsT", [P, NPAIR, L], F32, attn)
        x1 = sb("x1", [P, NT, D], F32, attn)
        wkv2 = sb("wkv2", [P, KD, 2, LD], F32, attn)
        wr = sb("wr", [P, KD, E], F32, attn)
        logit = sb("logit", [P, NT, E], F32, attn)
        work_a = sb("work_a", [P, NT, E], F32, attn)
        work_b = sb("work_b", [P, NT, E], F32, attn)
        onehot = sb("onehot", [P, NT, E], BF16, attn)
        earlier = sb("earlier", [P, NT, E], BF16, attn)
        in_tiles = sb("in_tiles", [P, E], F32, attn)
        rt = sb("rt", [P, 10, NT], F32, attn)
        send_idx = sb("send_idx", [P, NT], I32, attn)

        room = headsT[:, :, :].rearrange("p t d -> p (t d)")
        at = [0]

        def carve(cols):
            at[0] += cols
            return room[:, at[0] - cols:at[0]]

        wq_in = carve(KD * H * HD).rearrange("p (k n) -> p k n", k=KD)
        wqT = carve(NPAIR * D)
        wk_in = carve(H * HD)
        wv_in = carve(H * HD)
        wkT = carve(NPAIR * LD)
        wvT = carve(NPAIR * LD)
        wout_in = x1[:, :, :]
        ZR = 2
        zero_rows = carve(ZR * D)
        attn.close()

        tail = ExitStack()
        x1_all = sb("x1_all", [P, B * NT, D], F32, tail)
        ex_x = sb("ex_x", [P, 4, NB, D], F32, tail)
        ex_w = sb("ex_w", [P, 4, 3, 2, D], F32, tail)
        ex_xT = sb("ex_xT", [P, 4, KD, C], F32, tail)
        ex_s = sb("ex_s", [P, 4, KF, C], F32, tail)
        ex_h = sb("ex_h", [P, 4, KF, C], F32, tail)
        ex_y = sb("ex_y", [P, 4, NB, D], F32, tail)
        NL = 4
        LAST = B * NT // (2 * NL)
        last_y = sb("last_y", [P, 2 * NL, D], F32, tail)
        last_idx = sb("last_idx", [P, 2 * NL], I32, tail)
        last_o = sb("last_o", [P, 2 * NL, D], F32, tail)
        tail.close()

        const_ready = sem("const_ready")
        w_loaded = sem("w_loaded")
        zeroed = sem("zeroed")
        ring_full = sem("ring_full")
        ring_free = [sem(f"ring_free{i}") for i in range(NRING)]
        x_loaded = sem("x_loaded")
        xres_loaded = sem("xres_loaded")
        lat_hi_done = sem("lat_hi_done")
        fold_staged = sem("fold_staged")
        q_hi_done = sem("q_hi_done")
        score_full = sem("score_full")
        max_done = sem("max_done")
        exp_done = sem("exp_done")
        inverse_done = sem("inverse_done")
        probT_hi_done = sem("probT_hi_done")
        low_copied = sem("low_copied")
        dve_step = sem("dve_step")
        inverse_wide = sem("inverse_wide")
        normalised = sem("normalised")
        var_ready = sem("var_ready")
        rstd_ready = sem("rstd_ready")
        x1_ready = sem("x1_ready")
        x1_kept = sem("x1_kept")
        x1_back = sem("x1_back")
        logit_ready = sem("logit_ready")
        gate_exp = sem("gate_exp")
        onehot_ready = sem("onehot_ready")
        routed = sem("routed")
        send_ready = sem("send_ready")
        sent = sem("sent")
        ex_loaded = [sem(f"ex_loaded{i}") for i in range(4)]
        ex_t_full = sem("ex_t_full")
        ex_t_ready = sem("ex_t_ready")
        ex_g_full = sem("ex_g_full")
        ex_s_ready = sem("ex_s_ready")
        ex_h_ready = [sem(f"ex_h_ready{f}") for f in range(KF)]
        ex_y_full = sem("ex_y_full")
        ex_y_free = [sem(f"ex_y_free{i}") for i in range(2)]
        ex_stored = [sem(f"ex_stored{i}") for i in range(4)]
        idx_ready = sem("idx_ready")
        fetched = [sem(f"fetched{i}") for i in range(2)]
        last_ready = [sem(f"last_ready{i}") for i in range(2)]
        out_stored = [sem(f"out_stored{i}") for i in range(2)]

        PRIMED = 1
        primed = [normalised, x1_kept, ex_t_ready, *ex_h_ready, *ex_y_free, *ex_stored,
                  *last_ready, *out_stored]

        def numbered(uses):
            assert len(uses) % NRING == 0, len(uses)
            return {u: i for i, u in enumerate(uses)}

        SUMS_LAG = 3
        last_of = {c: max(k for k, i in enumerate(ORDER) if i // TPQ == c) for c in range(NQ)}
        SUMS_AT = {NT * h + k + SUMS_LAG: (h, c) for h in range(4) for c, k in last_of.items()}
        SUMS_LATE = [SUMS_AT[s] for s in sorted(SUMS_AT) if s >= NS]
        SUMS_ORDER = {SUMS_AT[s]: n for n, s in enumerate(sorted(SUMS_AT))}
        Q_AT = {1: (1, 0), 3: (1, 1), 17: (0, 0), 19: (0, 1)}
        NORM_STEP = 20
        probT_uses = lambda s: [("probT", s, c) for c, _ in chunks(STEPS[s][1])]
        setup_uses = ([("wqT", c) for c in range(4)] + [("wkT", 0), ("wvT", 0)]
                      + [("A", h, kd) for h in range(2) for kd in range(KD)]
                      + [("V", h, c) for h in range(2) for c in range(4)])
        start_uses = [("xT", c) for c in range(4)] + [(w, c) for w in ("lat", "lat_keys") for c in range(2)]
        FIRST = numbered(setup_uses + start_uses + [("q", 0, 0), ("q", 0, 1)])
        TURN = numbered(start_uses + [("proj", i) for i in range(NT)] + [("x1T", 0, kd) for kd in range(KD)]
                        + [("q", 0, 0)] + [("x1T", 1, kd) for kd in range(KD)] + [("logits", 0), ("q", 0, 1), ("pos", 0)])
        loop_uses = []
        for s in range(NS):
            if s >= 1:
                loop_uses += probT_uses(s - 1)
            if s in SUMS_AT:
                loop_uses += [("sums", *SUMS_AT[s])]
            if s in Q_AT:
                loop_uses += [("q", *Q_AT[s])]
            if s == NORM_STEP:
                loop_uses += [("rinv", 0, 0), ("rinv", 0, 1)]
        loop_uses += probT_uses(NS - 1) + [("sums", *SUMS_LATE[0]), ("rinv", 1, 0), ("rinv", 1, 1)]
        loop_uses += [("sums", *sums) for sums in SUMS_LATE[1:]]
        LOOP = numbered(loop_uses)
        PROBT_ORDER = {u: i for i, u in enumerate(u for u in loop_uses if u[0] == "probT")}
        N_CHUNKS = len(PROBT_ORDER)
        BATCH_USES = G * len(LOOP) + len(TURN)

        def ring_bases(b):
            loops = len(FIRST) + b * BATCH_USES
            return loops, loops + G * len(LOOP)

        def ring_rounds(b):
            loops = len(FIRST) // NRING + b * (BATCH_USES // NRING)
            return loops, loops + G * len(LOOP) // NRING

        END_STEPS = NT + 16

        def y_use(u, n):
            return (u * NB + n) % 2, (u * NB + n) // 2

        SCORED = G * NS + 2

        def transposed(probsT, s, c, n):
            quarter, t = divmod(STEPS[s][1], TPQ)
            return probsT[quarter][:, HPB * c:HPB * c + n, t * P:(t + 1) * P]

        block = ctx.enter_context(nc.Block())

        def wait_alone(eng, sem, value):
            eng.compute_val(value)
            eng.wait_ge(const_ready, 15)
            eng.wait_ge(sem, value)

        @block.sync
        def _(sp):
            for s in primed:
                sp.sem_inc(s, PRIMED)
            sp.dma_start(wq_in, Wq.rearrange("(k p) h e -> p k (h e)", p=P)).then_inc(w_loaded, 16)
            sp.dma_start(wk_in[0:LD, :], Wk_up.rearrange("c h e -> c (h e)")).then_inc(w_loaded, 16)
            sp.dma_start(wv_in[0:LD, :], Wv_up.rearrange("c h e -> c (h e)")).then_inc(w_loaded, 16)
            sp.dma_start(wout_in, Wout.rearrange("(j h) e o -> (h e) j o", h=2)).then_inc(w_loaded, 16)
            sp.dma_start(wkv2[:, :, 0, :], Wkv.rearrange("(k p) c -> p k c", p=P)).then_inc(w_loaded, 16)
            sp.dma_start(wkv2[:, :, 1, :], Wkv.rearrange("(k p) c -> p k c", p=P)).then_inc(w_loaded, 16)
            sp.dma_start(wr[:, :, :], w_router.rearrange("(k p) e -> p k e", p=P)).then_inc(w_loaded, 16)
            sp.wait_ge(const_ready, 1)
            zero_view = slots_x.rearrange("(n r p) d -> n p r d", r=ZR, p=P)
            for n in range(zero_view.shape[0]):
                sp.dma_start(zero_view[n], zero_rows.rearrange("p (r d) -> p r d", r=ZR)).then_inc(zeroed, 16)
            sp.dma_start(x_in[:, :, :], x_tiles[0]).then_inc(x_loaded, 16)
            sp.dma_start(x_res[:, :, :], x_tiles[0]).then_inc(xres_loaded, 16)
            with sp.Fori(0, B - 1) as b:
                sp.wait_ge(ring_full, ring_bases(b)[0])
                sp.dma_start(x_in[:, :, :], x_tiles[bass.ds(b + 1, 1)].rearrange("b p t d -> p (b t) d")
                             ).then_inc(x_loaded, 16)
                sp.wait_ge(x1_ready, (b + 1) * 2)
                sp.dma_start(x_res[:, :, :], x_tiles[bass.ds(b + 1, 1)].rearrange("b p t d -> p (b t) d")
                             ).then_inc(xres_loaded, 16)
                sp.dma_start(x1_tiles[bass.ds(b, 1)].rearrange("b p t d -> p (b t) d"), x1[:, :, :]
                             ).then_inc(x1_kept, 16)
            sp.wait_ge(ring_full, len(FIRST) + (B - 1) * BATCH_USES)
            sp.dma_start(x_in[:, :, :], x_tiles[0]).then_inc(x_loaded, 16)
            sp.wait_ge(x1_ready, B * 2)
            sp.dma_start(x1_tiles[B - 1], x1[:, :, :]).then_inc(x1_kept, 16)
            sp.wait_ge(sent, 16 * NT * B)
            sp.wait_ge(fold_staged, 2 + B * (2 * G + 2))
            sp.wait_ge(routed, B)
            sp.wait_ge(exp_done, B * SCORED + 2)
            sp.wait_ge(x1_kept, 16 * B + PRIMED)

            def load_experts(g, sub):
                for u in range(2):
                    e, k = g * 4 + (sub * 2 + u), sub * 2 + u
                    for m, w in enumerate((w_gate, w_up, w_down)):
                        sp.dma_start(ex_w[:, k, m], w[bass.ds(e, 1)].rearrange("e (k p) f -> p (e k) f", p=P)
                                     ).then_inc(ex_loaded[k], 16)
                    rows = slots_x.rearrange("(e c) d -> e c d", c=C)[bass.ds(e, 1)]
                    for n, (r0, nr) in enumerate(BLOCKS):
                        sp.dma_start(ex_x[0:nr, k, n, :], rows[:, r0:r0 + nr, :].rearrange("e p d -> p (e d)")
                                     ).then_inc(ex_loaded[k], 16)

            load_experts(0, 0)
            for b in range(B):
                sp.dma_start(x1_all[:, b * NT:(b + 1) * NT, :], x1_tiles[b]).then_inc(x1_back, 16)
            with sp.Fori(0, E // 4 - 1) as g:
                for i in range(2):
                    sp.wait_ge(ex_y_free[i], g * (2 * NB) + PRIMED)
                load_experts(g, 1)
                for i in range(2):
                    sp.wait_ge(ex_y_free[i], g * (2 * NB) + NB + PRIMED)
                load_experts(g + 1, 0)
            for i in range(2):
                sp.wait_ge(ex_y_free[i], (E // 4 - 1) * 2 * NB + PRIMED)
            load_experts(E // 4 - 1, 1)
            with sp.Fori(0, LAST) as g:
                for u in range(2):
                    sp.wait_ge(last_ready[u], g + 1 + PRIMED)
                    sp.dma_start(out_tiles[bass.ds((g * 2 + u) * NL, NL)].rearrange("t p d -> p t d"),
                                 last_o[:, u * NL:(u + 1) * NL, :]).then_inc(out_stored[u], 16)
            for u in range(2):
                sp.wait_ge(out_stored[u], 16 * LAST + PRIMED)

        @block.gpsimd
        def _(pool):
            nc.gpsimd.memset(zero_rows, 0.0).then_inc(const_ready, 1)
            nc.gpsimd.memset(fold_q[:, :, NPAIR * P:], 0.0).then_inc(const_ready, 1)
            nc.gpsimd.memset(low_sum[:, :, :], 0.0).then_inc(const_ready, 1)
            nc.gpsimd.memset(earlier[:, :, :], 0.0).then_inc(const_ready, 1)
            nc.gpsimd.memset(ident[:, :], 0.0).then_inc(const_ready, 1)
            nc.gpsimd.memset(future_bf[:, :], 0.0).then_inc(const_ready, 1)
            nc.gpsimd.memset(before_bf[:, :], 1.0).then_inc(const_ready, 1)
            nc.gpsimd.memset(ones_bf[:, :], 1.0).then_inc(const_ready, 1)
            nc.gpsimd.memset(minus_half[:, :], -0.5).then_inc(const_ready, 1)
            nc.gpsimd.iota(expert_i[:, :], [[1, E]], base=-E, channel_multiplier=0).then_inc(const_ready, 1)
            pool.wait_ge(const_ready, 10)
            nc.gpsimd.affine_select(out=ident[:, :], in_=ident[:, :], pattern=[[-1, P]], compare_op=ALU.not_equal,
                                    fill=1.0, base=0, channel_multiplier=1).then_inc(const_ready, 1)
            nc.gpsimd.affine_select(out=future_bf[:, :], in_=future_bf[:, :], pattern=[[-1, P]], compare_op=ALU.is_ge,
                                    fill=MASKED, base=0, channel_multiplier=1).then_inc(const_ready, 1)
            nc.gpsimd.affine_select(out=before_bf[:, :], in_=before_bf[:, :], pattern=[[1, P]], compare_op=ALU.is_gt,
                                    fill=0.0, base=0, channel_multiplier=-1).then_inc(const_ready, 1)
            nc.gpsimd.tensor_copy(expert_m[:, :], expert_i[:, :]).then_inc(const_ready, 1)
            pool.wait_ge(const_ready, 14)
            nc.gpsimd.tensor_copy(ident_bf[:, :], ident[:, :]).then_inc(const_ready, 1)
            for c in range(KD):
                n = FIRST[("A", 1, c)]
                pool.wait_ge(ring_free[n % NRING], n // NRING + 1)
            nc.gpsimd.tensor_copy(fold_stage[:, :, :], fold_q[:, :, 0:P]).then_inc(fold_staged, 1)
            pool.wait_ge(ring_full, len(FIRST))
            nc.gpsimd.tensor_copy(fold_stage[:, :, :], fold_q[:, :, P:2 * P]).then_inc(fold_staged, 1)
            pool.wait_ge(zeroed, 16 * (SLOTS // (ZR * P)))
            with pool.Fori(0, B) as b:
                with pool.Fori(0, G) as g:
                    base = pool.snap(ring_bases(b)[0] + g * len(LOOP))
                    rounds = pool.snap(ring_rounds(b)[0] + g * (len(LOOP) // NRING))
                    for q in range(2):
                        wait_alone(pool, ring_full, base + LOOP[("q", 1 - q, 1)] + 1)
                        nc.gpsimd.tensor_copy(fold_stage[:, :, :], fold_q[:, :, bass.ds((2 * g + 2 + q) * P, P)]
                                              ).then_inc(fold_staged, 1)
                        pair = (b * G + g) * 2 + q
                        wait_alone(pool, inverse_done, pair + 1)
                        for h in range(2):
                            ins = nc.gpsimd.tensor_copy(rinv_wide[:, :, h, :], rinv[:, 2 * q + h, :].unsqueeze(2).to_broadcast([P, NT, LD]))
                        ins.then_inc(inverse_wide, 1)
                        uses = [("rinv", q, c) for c in range(2)] + [("sums", 2 * q + h, c) for h in range(2) for c in range(NQ)]
                        for n in {n % NRING: n for n in sorted(LOOP[use] for use in uses)}.values():
                            wait_alone(pool, ring_free[n % NRING], rounds + n // NRING + 1)
                        dst = headsT[:, bass.ds(2 * g + q, 1), :].rearrange("p a n -> p (a n)")
                        nc.gpsimd.tensor_tensor(dst, dst, rinv_rows[:, :], ALU.mult).then_inc(normalised, 1)
                nc.gpsimd.tensor_copy(fold_stage[:, :, :], fold_q[:, :, 0:P]).then_inc(fold_staged, 1)
                for hf in range(2):
                    tiles = slice(hf * HPB, (hf + 1) * HPB)
                    wait_alone(pool, var_ready, b * 2 + (hf + 1))
                    nc.gpsimd.tensor_tensor(rstd[:, tiles], var_eps[:, tiles], minus_half[:, tiles], ALU.pow
                                            ).then_inc(rstd_ready, 1)
                wait_alone(pool, ring_full, ring_bases(b)[1] + TURN[("q", 0, 1)] + 1)
                nc.gpsimd.tensor_copy(fold_stage[:, :, :], fold_q[:, :, P:2 * P]).then_inc(fold_staged, 1)
                wait_alone(pool, send_ready, b + 1)
                for i in range(NT):
                    nc.gpsimd.indirect_dma_start(
                        out=slots_x, out_offset=bass.IndirectOffsetOnAxis(ap=send_idx[:, i:i + 1], axis=0),
                        in_=x1[:, i, :], in_offset=None, bounds_check=SLOTS - 1, oob_is_err=False).then_inc(sent, 16)
                wait_alone(pool, sent, (b + 1) * (16 * NT))
            for k in range(4):
                pool.wait_ge(ex_stored[k], 16 * NB * (E // 4) + PRIMED)
            def fetch(n, u):
                nc.gpsimd.tensor_copy(last_idx[:, u * NL:(u + 1) * NL], fetch_all[:, bass.ds(n * NL, NL)]
                                      ).then_inc(idx_ready, 1)
                wait_alone(pool, idx_ready, n + 1)
                for i in range(NL):
                    nc.gpsimd.indirect_dma_start(
                        out=last_y[:, u * NL + i, :], out_offset=None, in_=slots_y,
                        in_offset=bass.IndirectOffsetOnAxis(ap=last_idx[:, u * NL + i:u * NL + i + 1], axis=0),
                        bounds_check=SLOTS - 1, oob_is_err=False).then_inc(fetched[u], 16)

            def root(n, u):
                half_ = slice(u * NL, (u + 1) * NL)
                wait_alone(pool, var_ready, n + (2 * B + 1))
                nc.gpsimd.tensor_tensor(rstd[:, half_], var_eps[:, half_], minus_half[:, half_], ALU.pow
                                        ).then_inc(rstd_ready, 1)

            fetch(0, 0)
            with pool.Fori(0, LAST - 1) as g:
                wait_alone(pool, last_ready[1], g + PRIMED)
                fetch(g * 2 + 1, 1)
                root(g * 2, 0)
                wait_alone(pool, last_ready[0], g + 1 + PRIMED)
                fetch(g * 2 + 2, 0)
                root(g * 2 + 1, 1)
            wait_alone(pool, last_ready[1], LAST - 1 + PRIMED)
            fetch(LAST * 2 - 1, 1)
            root(LAST * 2 - 2, 0)
            root(LAST * 2 - 1, 1)

        @block.tensor
        def _(pe):
            rounds = {"first": 0}

            def ring_wait(part, uses, use):
                n = uses[use]
                pe.wait_ge(ring_free[n % NRING], rounds[part] + n // NRING)
                return ring[n % NRING]

            def evacuated(part, uses, use):
                n = uses[use]
                pe.wait_ge(ring_free[n % NRING], rounds[part] + n // NRING + 1)

            pe.wait_ge(const_ready, 15)
            pe.wait_ge(w_loaded, 16 * 7)
            for c in range(4):
                bank = ring_wait("first", FIRST, ("wqT", c))
                for k in range(4):
                    j, kd = 2 * c + k // 2, k % 2
                    mm = nc.tensor.transpose(bank[:, k * P:(k + 1) * P], wq_in[:, kd, j * P:(j + 1) * P], ident[:, :])
                mm.then_inc(ring_full, 1)
            for name, w in (("wkT", wk_in), ("wvT", wv_in)):
                bank = ring_wait("first", FIRST, (name, 0))
                for j in range(NPAIR):
                    mm = nc.tensor.transpose(bank[:, j * LD:(j + 1) * LD], w[0:LD, j * P:(j + 1) * P], ident[0:LD, 0:LD])
                mm.then_inc(ring_full, 1)
            for c in range(4):
                evacuated("first", FIRST, ("wqT", c))
            evacuated("first", FIRST, ("wkT", 0))
            evacuated("first", FIRST, ("wvT", 0))
            for h in range(2):
                rows = slice(h * HD, (h + 1) * HD)
                for kd in range(KD):
                    bank = ring_wait("first", FIRST, ("A", h, kd))
                    for j in range(NPAIR):
                        mm = nc.tensor.matmul(bank[:, j * LD:(j + 1) * LD],
                                              wqT[rows, j * D + kd * P:j * D + (kd + 1) * P],
                                              wkT[rows, j * LD:(j + 1) * LD], start=True, stop=True)
                    mm.then_inc(ring_full, 1)
            for h in range(2):
                rows = slice(h * HD, (h + 1) * HD)
                for c in range(4):
                    bank = ring_wait("first", FIRST, ("V", h, c))
                    for j in (2 * c, 2 * c + 1):
                        mm = nc.tensor.matmul(bank[rows, (j % 2) * D:(j % 2 + 1) * D], wvT[rows, j * LD:(j + 1) * LD],
                                              wout_in[rows, j, :], start=True, stop=True)
                    mm.then_inc(ring_full, 1)
            for c in range(4):
                evacuated("first", FIRST, ("V", 1, c))

            def project_q(base, uses, *use):
                bank = ring_wait(base, uses, ("q", *use))
                hf = use[-1]
                for kd in range(KD):
                    mm = nc.tensor.matmul(bank[:, :], fold_stage[:, kd, :], xT[:, kd, hf * BANK:(hf + 1) * BANK],
                                          start=(kd == 0), stop=(kd == KD - 1))
                mm.then_inc(ring_full, 1)

            def scores(s, scored0):
                h, i = STEPS[s % NS]
                if s >= 2:
                    pe.wait_ge(exp_done, scored0 + s - 1)
                keys = (i + 1) * P
                q = q_hl[:, h // 2, h % 2, i * P:(i + 1) * P]
                for k0 in range(0, keys, BANK):
                    k1 = min(keys, k0 + BANK)
                    dst = score_ps[s % 2]
                    nc.tensor.matmul(dst[:, k0:k1], q, lat_hi[:, k0:k1], start=True, stop=False)
                    if k1 == keys:
                        nc.tensor.matmul(dst[:, keys - P:keys], ident_bf[:, :], future_bf[:, :],
                                         start=False, stop=False)
                    mm = nc.tensor.matmul(dst[:, k0:k1], q, lat_lo[:, k0:k1], start=False, stop=True)
                mm.then_inc(score_full, 1)

            def transpose_x(base, uses):
                for c in range(4):
                    bank = ring_wait(base, uses, ("xT", c))
                    kd, t0 = c // 2, HPB * (c % 2)
                    for k in range(HPB):
                        mm = nc.tensor.transpose(bank[:, k * P:(k + 1) * P], x_in[:, t0 + k, kd * P:(kd + 1) * P],
                                                 ident[:, :])
                    mm.then_inc(ring_full, 1)

            def make_latents(base, uses):
                for hf in range(2):
                    evacuated(base, uses, ("xT", hf))
                    evacuated(base, uses, ("xT", 2 + hf))
                    bank = ring_wait(base, uses, ("lat", hf))
                    for kd in range(KD):
                        mm = nc.tensor.matmul(bank[:, :], wkv2[:, kd].rearrange("p a c -> p (a c)"),
                                              xT[:, kd, hf * BANK:(hf + 1) * BANK], start=(kd == 0), stop=(kd == KD - 1))
                    mm.then_inc(ring_full, 1)
                for hf in range(2):
                    bank = ring_wait(base, uses, ("lat_keys", hf))
                    for k in range(HPB):
                        i = hf * HPB + k
                        for kd in range(KD):
                            mm = nc.tensor.matmul(bank[:, k * LD:(k + 1) * LD], xT[:, kd, i * P:(i + 1) * P],
                                                  wkv2[:, kd, 0, :], start=(kd == 0), stop=(kd == KD - 1))
                    mm.then_inc(ring_full, 1)

            pe.wait_ge(x_loaded, 16)
            transpose_x("first", FIRST)
            make_latents("first", FIRST)
            pe.wait_ge(fold_staged, 1)
            for hf in range(2):
                project_q("first", FIRST, 0, hf)
            for use in [("lat", 1), ("lat_keys", 1), ("q", 0, 0), ("q", 0, 1)]:
                evacuated("first", FIRST, use)
            for s in range(2):
                scores(s, None)

            with pe.Fori(0, B) as b:
                with pe.Fori(0, G) as g:
                    rounds["loop"] = pe.snap(ring_rounds(b)[0] + g * (len(LOOP) // NRING))
                    pairs2 = b * G + g
                    scored0 = pe.snap(b * SCORED + g * NS)

                    def transpose_probs(s):
                        h, i = STEPS[s]
                        pe.wait_ge(exp_done, scored0 + s + 1)
                        for c, n in chunks(i):
                            bank = ring_wait("loop", LOOP, ("probT", s, c))
                            for k in range(n):
                                j = HPB * c + k
                                mm = nc.tensor.transpose(bank[:, k * P:(k + 1) * P],
                                                         probs[:, s % NPROBS, j * P:(j + 1) * P], ident[:, :])
                            mm.then_inc(ring_full, 1)

                    def spread_inverse(q):
                        pe.wait_ge(inverse_wide, pairs2 * 2 + q + 1)
                        for c in range(2):
                            bank = ring_wait("loop", LOOP, ("rinv", q, c))
                            for k in range(HPB):
                                i = HPB * c + k
                                mm = nc.tensor.transpose(bank[:, k * P:(k + 1) * P],
                                                         rinv_wide[:, i].rearrange("p a c -> p (a c)"),
                                                         ident[:, :])
                            mm.then_inc(ring_full, 1)

                    def times_latents(h, c):
                        last_use = {}
                        for s in range(h * NT, (h + 1) * NT):
                            if STEPS[s][1] // TPQ == c:
                                last_use.update({LOOP[use] % NRING: use for use in probT_uses(s)})
                        for n, use in last_use.items():
                            if n != LOOP[("sums", h, c)] % NRING:
                                evacuated("loop", LOOP, use)
                        bank = ring_wait("loop", LOOP, ("sums", h, c))
                        blocks = TPQ * (c + 1)
                        for j in range(blocks):
                            q0 = max(0, j - TPQ * c) * P
                            for part in (probsT_hi, probsT_lo):
                                mm = nc.tensor.matmul(bank[:, q0:QUARTER], lat_keys[:, j].rearrange("p a c -> p (a c)"),
                                                      part[c][:, j, q0:QUARTER], start=(j == 0 and part is probsT_hi),
                                                      stop=(j == blocks - 1 and part is probsT_lo))
                        mm.then_inc(ring_full, 1)

                    for s in range(NS):
                        scores(s + 2, scored0)
                        if s >= 1:
                            transpose_probs(s - 1)
                        if s in SUMS_AT:
                            times_latents(*SUMS_AT[s])
                        if s in Q_AT:
                            pair, hf = Q_AT[s]
                            pe.wait_ge(fold_staged, b * (2 * G + 2) + (g * 2 + 3 - pair))
                            project_q("loop", LOOP, pair, hf)
                        if s == NORM_STEP:
                            spread_inverse(0)
                    transpose_probs(NS - 1)
                    times_latents(*SUMS_LATE[0])
                    spread_inverse(1)
                    for sums in SUMS_LATE[1:]:
                        times_latents(*sums)

                rounds["turn"] = pe.snap(ring_rounds(b)[1])
                pe.wait_ge(x_loaded, (b + 2) * 16)
                transpose_x("turn", TURN)
                make_latents("turn", TURN)
                pe.wait_ge(normalised, (b + 1) * NPAIR + PRIMED)
                for i in range(NT):
                    bank = ring_wait("turn", TURN, ("proj", i))
                    for j in range(NPAIR):
                        mm = nc.tensor.matmul(bank[:, 0:D], headsT[:, j, i * P:(i + 1) * P], fold_v[:, j, :],
                                              start=(j == 0), stop=(j == NPAIR - 1))
                    mm.then_inc(ring_full, 1)

                def transpose_x1(hf):
                    pe.wait_ge(x1_ready, b * 2 + (hf + 1))
                    for kd in range(KD):
                        bank = ring_wait("turn", TURN, ("x1T", hf, kd))
                        for k in range(HPB):
                            mm = nc.tensor.transpose(bank[:, k * P:(k + 1) * P],
                                                     x1[:, hf * HPB + k, kd * P:(kd + 1) * P], ident[:, :])
                        mm.then_inc(ring_full, 1)

                transpose_x1(0)
                pe.wait_ge(fold_staged, b * (2 * G + 2) + (2 * G + 3))
                project_q("turn", TURN, 0, 0)
                transpose_x1(1)
                for kd in range(KD):
                    evacuated("turn", TURN, ("x1T", 1, kd))
                bank = ring_wait("turn", TURN, ("logits", 0))
                for i in range(NT):
                    for kd in range(KD):
                        mm = nc.tensor.matmul(bank[:, i * E:(i + 1) * E], x1T[:, kd, i * P:(i + 1) * P],
                                              wr[:, kd, :], start=(kd == 0), stop=(kd == KD - 1))
                mm.then_inc(ring_full, 1)
                project_q("turn", TURN, 0, 1)
                bank = ring_wait("turn", TURN, ("pos", 0))
                pe.wait_ge(onehot_ready, b + 1)
                nc.tensor.matmul(bank[:, 0:NT * E], before_bf[:, :], onehot[:, :, :].rearrange("p t e -> p (t e)"),
                                 start=True, stop=False)
                for d in range(1, NT):
                    nc.tensor.matmul(bank[:, d * E:NT * E], ones_bf[:, :],
                                     onehot[:, 0:NT - d, :].rearrange("p t e -> p (t e)"), start=False, stop=False)
                nc.tensor.matmul(bank[:, 0:NT * E], ones_bf[:, :], earlier[:, :, :].rearrange("p t e -> p (t e)"),
                                 start=False, stop=True).then_inc(ring_full, 1)
                evacuated("turn", TURN, ("q", 0, 1))
                for s in range(2):
                    scores(s, None)

            pe.wait_ge(routed, B)
            pe.wait_ge(exp_done, B * SCORED + 2)
            with pe.Fori(0, E // 4) as g:
                for sub in range(2):
                    for u in range(2):
                        k, e = sub * 2 + u, g * 4 + (sub * 2 + u)
                        pe.wait_ge(ex_loaded[k], (g + 1) * (16 * (3 + NB)))
                        pe.wait_ge(ex_t_ready, e + PRIMED)
                        for kd in range(KD):
                            for n, (r0, nr) in enumerate(BLOCKS):
                                mm = nc.tensor.transpose(ring[kd][:, r0:r0 + nr], ex_x[0:nr, k, n, kd * P:(kd + 1) * P],
                                                         ident[0:nr, 0:nr])
                        mm.then_inc(ex_t_full, 1)
                    for u in range(2):
                        k, e = sub * 2 + u, g * 4 + (sub * 2 + u)
                        pe.wait_ge(ex_t_ready, e + 1 + PRIMED)
                        for f in range(KF):
                            pe.wait_ge(ex_h_ready[f], e + PRIMED)
                            for m in range(2):
                                for kd in range(KD):
                                    mm = nc.tensor.matmul(score_ps[f][:, m * BANK:m * BANK + C],
                                                          ex_w[:, k, m, kd, f * P:(f + 1) * P], ex_xT[:, k, kd, :],
                                                          start=(kd == 0), stop=(kd == KD - 1))
                            mm.then_inc(ex_g_full, 1)
                    for u in range(2):
                        k, e = sub * 2 + u, g * 4 + (sub * 2 + u)
                        for f in range(KF):
                            pe.wait_ge(ex_h_ready[f], e + 1 + PRIMED)
                        for n, (r0, nr) in enumerate(BLOCKS):
                            bank, uses = y_use(u, n)
                            pe.wait_ge(ex_y_free[bank], g * (2 * NB) + (sub * NB + uses) + PRIMED)
                            for f in range(KF):
                                mm = nc.tensor.matmul(ring[2 + bank][0:nr, 0:D], ex_h[:, k, f, r0:r0 + nr],
                                                      ex_w[:, k, 2, f, :], start=(f == 0), stop=(f == KF - 1))
                            mm.then_inc(ex_y_full, 1)

        @block.scalar
        def _(act):
            def full(base, uses, use):
                n = uses[use]
                act.wait_ge(ring_full, base + n + 1)
                return ring[n % NRING], ring_free[n % NRING]

            for name, dst in (("wkT", wkT), ("wvT", wvT)):
                bank, done = full(0, FIRST, (name, 0))
                nc.scalar.copy(dst, bank[:, :]).then_inc(done, 1)
            for h in range(2):
                rows = slice(h * HD, (h + 1) * HD)
                for c in range(4):
                    bank, done = full(0, FIRST, ("V", h, c))
                    nc.scalar.copy(fold_v[rows, 2 * c:2 * c + 2, :].rearrange("p j n -> p (j n)"), bank[rows, :]
                                   ).then_inc(done, 1)

            def split_hi(base, uses, pair, *use):
                bank, _ = full(base, uses, ("q", *use))
                cols = slice(use[-1] * BANK, (use[-1] + 1) * BANK)
                nc.scalar.copy(q_hl[0:64, pair, 0, cols], bank[0:64, :])
                nc.scalar.copy(q_hl[64:128, pair, 1, cols], bank[64:128, :]).then_inc(q_hi_done, 1)

            def high_of_start(base, uses):
                for c in (1, 3):
                    bank, done = full(base, uses, ("xT", c))
                    nc.scalar.copy(xT[:, c // 2, (c % 2) * BANK:(c % 2 + 1) * BANK], bank[:, :]).then_inc(done, 1)
                for hf in range(2):
                    bank, _ = full(base, uses, ("lat", hf))
                    nc.scalar.copy(lat_hi[:, hf * BANK:(hf + 1) * BANK], bank[:, :]).then_inc(lat_hi_done, 1)
                for hf in range(2):
                    bank, _ = full(base, uses, ("lat_keys", hf))
                    nc.scalar.copy(lat_keys[:, hf * HPB:(hf + 1) * HPB, 0, :],
                                   bank[:, 0:HPB * LD].rearrange("p (t c) -> p t c", c=LD)).then_inc(lat_hi_done, 1)

            def exponentials(s, scored0, base):
                keys = (STEPS[s % NS][1] + 1) * P
                act.wait_ge(max_done, scored0 + s + 1)
                if s >= NPROBS:
                    act.wait_ge(ring_full, base + LOOP[probT_uses(s - NPROBS)[-1]] + 1)
                nc.scalar.activation(probs[:, s % NPROBS, 0:keys], score_ps[s % 2][:, 0:keys], ACT.Exp,
                                     bias=negmax[:, s % NS:s % NS + 1],
                                     accum_out=rowsum[:, STEPS[s % NS][0], STEPS[s % NS][1]:STEPS[s % NS][1] + 1]
                                     ).then_inc(exp_done, 1)

            high_of_start(0, FIRST)
            for hf in range(2):
                split_hi(0, FIRST, 0, 0, hf)
            for s in range(2):
                exponentials(s, 0, None)

            with act.Fori(0, B) as b:
                loops, turn = ring_bases(b)
                with act.Fori(0, G) as g:
                    base = act.snap(loops + g * len(LOOP))
                    scored0 = act.snap(b * SCORED + g * NS)

                    def copy_low(h, c):
                        bank, _ = full(base, LOOP, ("sums", h, c))
                        nc.scalar.copy(low_sum[0:LD, c, :], bank[LD:2 * LD, 0:QUARTER]).then_inc(low_copied, 1)

                    def copy_inverse(q):
                        act.wait_ge(normalised, (b * G + g) * 2 + (q + PRIMED))
                        for c in range(2):
                            bank, done = full(base, LOOP, ("rinv", q, c))
                            nc.scalar.copy(rinv_rows[:, c * BANK:(c + 1) * BANK], bank[:, :]).then_inc(done, 1)

                    def high_parts(s):
                        h, i = STEPS[s]
                        if h >= 1:
                            act.wait_ge(ring_full, base + LOOP[("sums", h - 1, i // TPQ)] + 1)
                        for c, n in chunks(i):
                            bank, _ = full(base, LOOP, ("probT", s, c))
                            nc.scalar.copy(transposed(probsT_hi, s, c, n),
                                           bank[:, 0:n * P].rearrange("p (k q) -> p k q", k=n)).then_inc(probT_hi_done, 1)

                    for s in range(NS + 2):
                        if s >= 2:
                            exponentials(s, scored0, base)
                        if s >= HI_LAG:
                            high_parts(s - HI_LAG)
                        if s - 1 in Q_AT:
                            split_hi(base, LOOP, Q_AT[s - 1][0], *Q_AT[s - 1])
                        if s - 1 == NORM_STEP:
                            copy_inverse(0)
                        if s - 1 < NS and s - 1 in SUMS_AT:
                            copy_low(*SUMS_AT[s - 1])
                    copy_low(*SUMS_LATE[0])
                    copy_inverse(1)
                    for sums in SUMS_LATE[1:]:
                        copy_low(*sums)

                turn = act.snap(turn)
                high_of_start(turn, TURN)

                def copy_x1T(hf):
                    for kd in range(KD):
                        bank, done = full(turn, TURN, ("x1T", hf, kd))
                        nc.scalar.copy(x1T[:, kd, hf * BANK:(hf + 1) * BANK], bank[:, :]).then_inc(done, 1)

                copy_x1T(0)
                split_hi(turn, TURN, 0, 0, 0)
                copy_x1T(1)
                split_hi(turn, TURN, 0, 0, 1)
                act.wait_ge(logit_ready, b + 1)
                nc.scalar.activation(work_b[:, :, :], work_a[:, :, :], ACT.Exp).then_inc(gate_exp, 1)
                for s in range(2):
                    exponentials(s, b * SCORED + SCORED, None)

            with act.Fori(0, E // 4) as g:
                for sub in range(2):
                    for u in range(2):
                        k, e = sub * 2 + u, g * 4 + (sub * 2 + u)
                        act.wait_ge(ex_t_full, e + 1)
                        nc.scalar.copy(ex_xT[:, k, 0, :], ring[0][:, 0:C])
                        nc.scalar.copy(ex_xT[:, k, 1, :], ring[1][:, 0:C]).then_inc(ex_t_ready, 1)
                    for u in range(2):
                        k, e = sub * 2 + u, g * 4 + (sub * 2 + u)
                        for f in range(KF):
                            act.wait_ge(ex_g_full, e * KF + (f + 1))
                            nc.scalar.activation(ex_s[:, k, f, :], score_ps[f][:, 0:C], ACT.Silu).then_inc(ex_s_ready, 1)
                    for u in range(2):
                        k, e = sub * 2 + u, g * 4 + (sub * 2 + u)
                        for n in range(max(0, NB - 2), NB):
                            bank, uses = y_use(u, n)
                            act.wait_ge(ex_y_free[bank], g * (2 * NB) + (sub * NB + uses + 1) + PRIMED)
                        rows = slots_y.rearrange("(e c) d -> e c d", c=C)[bass.ds(e, 1)]
                        for n, (r0, nr) in enumerate(BLOCKS):
                            act.dma_start(rows[:, r0:r0 + nr, :].rearrange("e p d -> p (e d)"), ex_y[0:nr, k, n, :]
                                          ).then_inc(ex_stored[k], 16)

        @block.vector
        def _(dve):
            def full(base, uses, use):
                n = uses[use]
                dve.wait_ge(ring_full, base + n + 1)
                return ring[n % NRING], ring_free[n % NRING]

            steps = [0, 0]

            def step(ins):
                steps[1] += 1
                ins.then_inc(dve_step, 1)

            def settle(alone=False):
                if alone:
                    wait_alone(dve, dve_step, steps[0] + steps[1])
                else:
                    dve.wait_ge(dve_step, steps[0] + steps[1])

            for c in range(4):
                bank, done = full(0, FIRST, ("wqT", c))
                nc.vector.tensor_copy(wqT[:, c * BANK:(c + 1) * BANK], bank[:, :]).then_inc(done, 1)
            for h in range(2):
                for kd in range(KD):
                    bank, done = full(0, FIRST, ("A", h, kd))
                    dst = fold_q[:, kd, 0:NPAIR * P].rearrange("p (j h c) -> p j h c", h=2, c=LD)[:, :, h, :]
                    nc.vector.tensor_scalar(dst, bank[:, :].rearrange("p (j c) -> p j c", c=LD),
                                            float(HD) ** -0.5, None, ALU.mult).then_inc(done, 1)

            def split_lo(base, uses, pair, count, *use):
                dve.wait_ge(q_hi_done, count + use[-1] + 1)
                bank, done = full(base, uses, ("q", *use))
                cols = slice(use[-1] * BANK, (use[-1] + 1) * BANK)
                nc.vector.tensor_tensor(q_hl[64:128, pair, 0, cols], bank[0:64, :], q_hl[0:64, pair, 0, cols].bitcast(F32),
                                        ALU.subtract)
                nc.vector.tensor_tensor(q_hl[0:64, pair, 1, cols], bank[64:128, :], q_hl[64:128, pair, 1, cols].bitcast(F32),
                                        ALU.subtract).then_inc(done, 1)

            def row_max(s, scored0):
                keys = (STEPS[s % NS][1] + 1) * P
                dve.wait_ge(score_full, scored0 + s + 1)
                nc.vector.tensor_reduce(negmax[:, s % NS:s % NS + 1], score_ps[s % 2][:, 0:keys], AX.X, ALU.max,
                                        negate=True).then_inc(max_done, 1)

            dve.wait_ge(zeroed, 16 * (SLOTS // (ZR * P)))
            def low_of_start(base, uses, n):
                for c in (0, 2):
                    bank, done = full(base, uses, ("xT", c))
                    nc.vector.tensor_copy(xT[:, c // 2, (c % 2) * BANK:(c % 2 + 1) * BANK], bank[:, :]).then_inc(done, 1)
                for hf in range(2):
                    dve.wait_ge(lat_hi_done, n * 4 + (hf + 1))
                    bank, done = full(base, uses, ("lat", hf))
                    cols = slice(hf * BANK, (hf + 1) * BANK)
                    nc.vector.tensor_tensor(lat_lo[:, cols], bank[:, :], lat_hi[:, cols].bitcast(F32), ALU.subtract
                                            ).then_inc(done, 1)
                for hf in range(2):
                    dve.wait_ge(lat_hi_done, n * 4 + (hf + 3))
                    bank, done = full(base, uses, ("lat_keys", hf))
                    tiles = slice(hf * HPB, (hf + 1) * HPB)
                    nc.vector.tensor_tensor(lat_keys[:, tiles, 1, :],
                                            bank[:, 0:HPB * LD].rearrange("p (t c) -> p t c", c=LD),
                                            lat_keys[:, tiles, 0, :].bitcast(F32), ALU.subtract).then_inc(done, 1)

            low_of_start(0, FIRST, 0)
            for hf in range(2):
                split_lo(0, FIRST, 0, 0, 0, hf)
            for s in range(2):
                row_max(s, 0)

            with dve.Fori(0, B) as b:
                loops, turn = ring_bases(b)
                with dve.Fori(0, G) as g:
                    base = dve.snap(loops + g * len(LOOP))
                    scored0 = dve.snap(b * SCORED + g * NS)
                    chunk0 = dve.snap((b * G + g) * N_CHUNKS)

                    def low_parts(s):
                        for c, n in chunks(STEPS[s][1]):
                            dve.wait_ge(probT_hi_done, chunk0 + PROBT_ORDER[("probT", s, c)] + 1)
                            bank, done = full(base, LOOP, ("probT", s, c))
                            nc.vector.tensor_tensor(transposed(probsT_lo, s, c, n),
                                                    bank[:, 0:n * P].rearrange("p (k q) -> p k q", k=n),
                                                    transposed(probsT_hi, s, c, n).bitcast(F32), ALU.subtract
                                                    ).then_inc(done, 1)

                    def add_sums(h, c):
                        dve.wait_ge(low_copied, (b * G + g) * (4 * NQ) + (SUMS_ORDER[(h, c)] + 1))
                        bank, done = full(base, LOOP, ("sums", h, c))
                        pair = bass.ds(2 * g + h // 2, 1)
                        cols = slice(c * QUARTER, (c + 1) * QUARTER)
                        nc.vector.tensor_tensor(
                            headsT[(h % 2) * LD:(h % 2 + 1) * LD, pair, cols].rearrange("p a n -> p (a n)"),
                            bank[0:LD, 0:QUARTER], low_sum[0:LD, c, :], ALU.add).then_inc(done, 1)

                    for s in range(NS + LO_LAG):
                        if 2 <= s < NS + 2:
                            row_max(s, scored0)
                        if s in (NS // 2, NS):
                            q = 2 * s // NS - 1
                            dve.wait_ge(exp_done, scored0 + s)
                            nc.vector.reciprocal(rinv[:, 2 * q:2 * q + 2, :], rowsum[:, 2 * q:2 * q + 2, :]
                                                 ).then_inc(inverse_done, 1)
                        if s >= LO_LAG:
                            low_parts(s - LO_LAG)
                        if s - 2 < NS and s - 2 in SUMS_AT:
                            add_sums(*SUMS_AT[s - 2])
                        if s - 2 in Q_AT:
                            pair, hf = Q_AT[s - 2]
                            split_lo(base, LOOP, pair, b * (4 * G + 2) + (4 * g + 4 - 2 * pair), pair, hf)
                    for sums in SUMS_LATE:
                        add_sums(*sums)

                turn = dve.snap(turn)
                turn_rounds = dve.snap(ring_rounds(b)[1])
                steps[0] = dve.snap(b * END_STEPS)
                steps[1] = 0

                def own(use):
                    n = TURN[use]
                    dve.wait_ge(ring_free[n % NRING], turn_rounds + (n // NRING + 1))

                low_of_start(turn, TURN, b + 1)
                dve.wait_ge(xres_loaded, (b + 1) * 16)
                dve.wait_ge(x1_kept, b * 16 + PRIMED)

                def add_and_count(i, h0):
                    bank, done = full(turn, TURN, ("proj", i))
                    nc.vector.tensor_tensor(x1[:, i, :], bank[:, 0:D], x_res[:, i, :], ALU.add).then_inc(done, 1)
                    if i > h0:
                        statistics(i - 1)

                def statistics(i):
                    own(("proj", i))
                    step(nc.vector.bn_stats(stat6[:, i, :], x1[:, i, :]))

                def variance(hf):
                    settle(alone=True)
                    for i in range(hf * HPB, (hf + 1) * HPB):
                        last = nc.vector.bn_aggr(mean_var[:, i, :], stat6[:, i, :])
                    step(last)
                    settle()
                    nc.vector.tensor_scalar(var_eps[:, hf * HPB:(hf + 1) * HPB], mean_var[:, hf * HPB:(hf + 1) * HPB, 1],
                                            EPS, None, ALU.add).then_inc(var_ready, 1)

                def normalise(hf):
                    dve.wait_ge(rstd_ready, b * 2 + (hf + 1))
                    for i in range(hf * HPB, (hf + 1) * HPB):
                        last = nc.vector.tensor_scalar(x1[:, i, :], x1[:, i, :], mean_var[:, i, 0:1], rstd[:, i:i + 1],
                                                       ALU.subtract, ALU.mult)
                    last.then_inc(x1_ready, 1)

                for i in range(HPB):
                    add_and_count(i, 0)
                statistics(HPB - 1)
                variance(0)
                add_and_count(HPB, HPB)
                normalise(0)
                for i in range(HPB + 1, NT):
                    add_and_count(i, HPB)
                statistics(NT - 1)
                variance(1)
                normalise(1)
                split_lo(turn, TURN, 0, (b + 1) * (4 * G + 2), 0, 0)
                over = lambda k: rt[:, k, :].unsqueeze(2).to_broadcast([P, NT, E])
                each = expert_m[:, :].unsqueeze(1).to_broadcast([P, NT, E])
                bank, done = full(turn, TURN, ("logits", 0))
                nc.vector.tensor_copy(logit[:, :, :].rearrange("p t e -> p (t e)"), bank[:, 0:NT * E]).then_inc(done, 1)
                own(("logits", 0))
                step(nc.vector.tensor_reduce(rt[:, 0, :], logit[:, :, :], AX.X, ALU.max))
                settle()
                nc.vector.tensor_tensor(work_a[:, :, :], logit[:, :, :], over(0), ALU.subtract).then_inc(logit_ready, 1)
                step(nc.vector.tensor_tensor(logit[:, :, :], logit[:, :, :], over(0), ALU.is_equal))
                settle()
                step(nc.vector.tensor_tensor(logit[:, :, :], logit[:, :, :], each, ALU.mult))
                settle()
                step(nc.vector.tensor_reduce(rt[:, 3, :], logit[:, :, :], AX.X, ALU.min))
                settle()
                nc.vector.tensor_tensor(onehot[:, :, :], each, over(3), ALU.is_equal).then_inc(onehot_ready, 1)
                split_lo(turn, TURN, 0, (b + 1) * (4 * G + 2), 0, 1)
                for s in range(2):
                    row_max(s, b * SCORED + SCORED)
                dve.wait_ge(gate_exp, b + 1)
                step(nc.vector.tensor_reduce(rt[:, 1, :], work_b[:, :, :], AX.X, ALU.add))
                settle()
                step(nc.vector.reciprocal(rt[:, 2, :], rt[:, 1, :]))
                bank, done = full(turn, TURN, ("pos", 0))
                nc.vector.tensor_tensor(work_a[:, :, :], onehot[:, :, :],
                                        bank[:, 0:NT * E].rearrange("p (t e) -> p t e", e=E), ALU.mult).then_inc(done, 1)
                own(("pos", 0))
                step(nc.vector.tensor_reduce(in_tiles[:, :], onehot[:, :, :].rearrange("p t e -> p e t"), AX.X, ALU.add))
                settle()
                step(nc.vector.tensor_tensor(earlier[:, :, :], earlier[:, :, :],
                                             in_tiles[:, :].unsqueeze(1).to_broadcast([P, NT, E]), ALU.add))
                step(nc.vector.tensor_reduce(rt[:, 4, :], work_a[:, :, :], AX.X, ALU.add))
                settle()
                step(nc.vector.scalar_tensor_tensor(rt[:, 5, :], rt[:, 3, :], float(C), rt[:, 4, :], ALU.mult, ALU.add))
                step(nc.vector.tensor_scalar(rt[:, 6, :], rt[:, 4, :], float(C), None, ALU.is_lt))
                step(nc.vector.tensor_scalar(rt[:, 7, :], rt[:, 4, :], float(C), FAR, ALU.is_ge, ALU.mult))
                settle()
                step(nc.vector.scalar_tensor_tensor(rt[:, 8, :], rt[:, 5, :], float(SLOTS), rt[:, 7, :], ALU.add, ALU.add))
                step(nc.vector.tensor_tensor(gate_all[:, bass.ds(b * NT, NT)], rt[:, 2, :], rt[:, 6, :], ALU.mult))
                settle()
                nc.vector.tensor_scalar(fetch_all[:, bass.ds(b * NT, NT)], rt[:, 8, :], float(SLOTS - 1), None, ALU.min
                                        ).then_inc(routed, 1)
                nc.vector.tensor_copy(send_idx[:, :], rt[:, 8, :]).then_inc(send_ready, 1)
                assert steps[1] == END_STEPS, steps

            with dve.Fori(0, E // 4) as g:
                for sub in range(2):
                    for u in range(2):
                        k, e = sub * 2 + u, g * 4 + (sub * 2 + u)
                        for f in range(KF):
                            dve.wait_ge(ex_s_ready, e * KF + (f + 1))
                            nc.vector.tensor_tensor(ex_h[:, k, f, :], ex_s[:, k, f, :], score_ps[f][:, BANK:BANK + C],
                                                    ALU.mult).then_inc(ex_h_ready[f], 1)
                    for u in range(2):
                        k, e = sub * 2 + u, g * 4 + (sub * 2 + u)
                        dve.wait_ge(ex_stored[k], g * (16 * NB) + PRIMED)
                        for n, (r0, nr) in enumerate(BLOCKS):
                            bank, _ = y_use(u, n)
                            dve.wait_ge(ex_y_full, e * NB + (n + 1))
                            nc.vector.tensor_copy(ex_y[0:nr, k, n, :], ring[2 + bank][0:nr, 0:D]
                                                  ).then_inc(ex_y_free[bank], 1)

            dve.wait_ge(x1_back, 16 * B)
            with dve.Fori(0, LAST) as g:
                steps[0] = dve.snap(B * END_STEPS + g * (2 * 4))
                steps[1] = 0
                for u in range(2):
                    n = g * 2 + u
                    half_ = slice(u * NL, (u + 1) * NL)
                    dve.wait_ge(fetched[u], (g + 1) * (16 * NL))
                    step(nc.vector.tensor_tensor(last_y[:, half_, :], last_y[:, half_, :],
                                                 gate_all[:, bass.ds(n * NL, NL)].unsqueeze(2).to_broadcast([P, NL, D]),
                                                 ALU.mult))
                    settle()
                    step(nc.vector.scalar_tensor_tensor(last_y[:, half_, :], x1_all[:, bass.ds(n * NL, NL), :], 2.0,
                                                        last_y[:, half_, :], ALU.mult, ALU.add))
                    settle()
                    for i in range(NL):
                        last = nc.vector.bn_stats(stat6[:, u * NL + i, :], last_y[:, u * NL + i, :])
                    step(last)
                    settle(alone=True)
                    for i in range(NL):
                        last = nc.vector.bn_aggr(mean_var[:, u * NL + i, :], stat6[:, u * NL + i, :])
                    step(last)
                    settle()
                    nc.vector.tensor_scalar(var_eps[:, half_], mean_var[:, half_, 1], EPS, None, ALU.add
                                            ).then_inc(var_ready, 1)
                    dve.wait_ge(rstd_ready, n + (2 * B + 1))
                    dve.wait_ge(out_stored[u], g * 16 + PRIMED)
                    for i in range(NL):
                        k = u * NL + i
                        last = nc.vector.tensor_scalar(last_o[:, k, :], last_y[:, k, :], mean_var[:, k, 0:1],
                                                       rstd[:, k:k + 1], ALU.subtract, ALU.mult)
                    last.then_inc(last_ready[u], 1)


_INS = ["L0_attn_x_bld", "L0_attn_Wq", "L0_attn_Wkv_down", "L0_attn_Wk_up", "L0_attn_Wv_up", "L0_attn_Wout",
        "L0_ffn_w_router", "L0_ffn_w_gate", "L0_ffn_w_up", "L0_ffn_w_down"]
_OUT = "layer_out"


def kernel(**inputs):
    import concourse.bacc as bacc
    from concourse.bass_utils import run_bass_kernel_spmd

    nc = bacc.Bacc("TRN2", target_bir_lowering=False, num_devices=1)
    arrays, aps = {}, []
    for name in _INS:
        a = np.ascontiguousarray(inputs[name])
        arrays["in_" + name] = a
        aps.append(nc.dram_tensor("in_" + name, a.shape, mybir.dt.from_np(a.dtype), kind="ExternalInput").ap())
    aps.append(nc.dram_tensor(_OUT, inputs["L0_attn_x_bld"].shape, F32, kind="ExternalOutput").ap())
    build_layer(nc, *aps)
    result = run_bass_kernel_spmd(nc, [arrays], core_ids=[0])
    return result.results[0][_OUT]
```

```python
import math
from contextlib import ExitStack

import numpy as np

import concourse.bass as bass
from concourse import mybir

ALU = mybir.AluOpType
ACT = mybir.ActivationFunctionType
AX = mybir.AxisListType
F32 = mybir.dt.float32
F32R = mybir.dt.float32r
BF16 = mybir.dt.bfloat16
I32 = mybir.dt.int32

P = 128
BANK = 512
EPS = 1e-5
MASKED = -1e30
FAR = 2.0 ** 22


def build_layer(nc, x, Wq, Wkv, Wk_up, Wv_up, Wout, w_router, w_gate, w_up, w_down, out):
    B, L, D = x.shape
    _, H, HD = Wq.shape
    LD = Wkv.shape[1]
    E, _, F = w_gate.shape
    T = B * L
    C = int(math.ceil(1.25 * T / E))
    NT = L // P
    NPAIR = H // 2
    KD = D // P
    KF = F // P
    HPB = BANK // P
    assert HD == 64 and LD == 64 and KD == 2 and KF == 2 and NT == 8 and D == 256 and C <= BANK
    SLOTS = E * C
    BLOCKS = [(r, min(P, C - r)) for r in range(0, C, P)]
    NB = len(BLOCKS)

    ORDER = [6, 7, 3, 2, 5, 4, 1, 0]
    STEPS = [(h, i) for h in range(4) for i in ORDER]
    NS = len(STEPS)
    G = NPAIR // 2
    TPQ = 2
    NQ = NT // TPQ
    QUARTER = TPQ * P
    AHEAD = 8
    assert E % AHEAD == 0
    HI_LAG, LO_LAG = 2, 3
    NRING = 4
    NPROBS = 4
    chunks = lambda i: [(c, min(HPB, i + 1 - HPB * c)) for c in range((i + HPB) // HPB)]

    slots_x = nc.dram_tensor("slots_x", [SLOTS, D], F32, kind="Internal").ap()
    x1_rows = nc.dram_tensor("x1_rows", [T, D], F32, kind="Internal").ap()
    slots_y = nc.dram_tensor("slots_y", [SLOTS, D], F32, kind="Internal").ap()
    x_tiles = x.rearrange("b (t p) d -> b p t d", p=P)
    x1_tiles = x1_rows.rearrange("(b t p) d -> b p t d", t=NT, p=P)
    out_tiles = out.rearrange("b (t p) d -> (b t) p d", p=P)

    with ExitStack() as ctx:
        def sb(name, shape, dt=F32, stack=ctx):
            return stack.enter_context(nc.sbuf_tensor(name, shape, dt))

        def sem(name):
            return ctx.enter_context(nc.semaphore(name))

        score_ps = [ctx.enter_context(nc.psum_tensor(f"score_ps{i}", [P, 2 * BANK], F32)) for i in range(2)]
        ring = [ctx.enter_context(nc.psum_tensor(f"ring{i}", [P, BANK], F32)) for i in range(NRING)]

        gate_all = sb("gate_all", [P, B * NT])
        fetch_all = sb("fetch_all", [P, B * NT], I32)
        ident = sb("ident", [P, P])
        stat6 = sb("stat6", [P, 16, 6])
        mean_var = sb("mean_var", [P, 16, 2])
        var_eps = sb("var_eps", [P, 16])
        rstd = sb("rstd", [P, 16])
        minus_half = sb("minus_half", [P, 16])

        attn = ExitStack()
        ident_bf = sb("ident_bf", [P, P], BF16, attn)
        future_bf = sb("future_bf", [P, P], BF16, attn)
        before_bf = sb("before_bf", [P, P], BF16, attn)
        ones_bf = sb("ones_bf", [P, P], BF16, attn)
        expert_m = sb("expert_m", [P, E], F32, attn)
        expert_i = sb("expert_i", [P, E], I32, attn)
        x_in = sb("x_in", [P, NT, D], F32, attn)
        x_res = sb("x_res", [P, NT, D], F32, attn)
        xT_hi = sb("xT_hi", [P, KD, L], F32R, attn)
        xT_lo = sb("xT_lo", [P, KD, L], F32R, attn)
        lat_hi = sb("lat_hi", [P, L], F32R, attn)
        lat_lo = sb("lat_lo", [P, L], F32R, attn)
        lat_keys = sb("lat_keys", [P, NT, 2, LD], F32R, attn)
        fold_q = sb("fold_q", [P, KD, (NPAIR + 2) * P], F32, attn)
        stage_hi = sb("stage_hi", [P, KD, P], F32R, attn)
        stage_lo = sb("stage_lo", [P, KD, P], F32R, attn)
        fold_v = sb("fold_v", [P, NPAIR, D], F32, attn)
        q_hl = sb("q_hl", [P, 2, 2, L], F32R, attn)
        probs = sb("probs", [P, NPROBS, L], F32, attn)
        x1T = probs[:, NPROBS - KD:NPROBS, :]
        probsT_hi = [sb(f"probsT_hi{c}", [P, TPQ * (c + 1), QUARTER], F32R, attn) for c in range(NQ)]
        probsT_lo = [sb(f"probsT_lo{c}", [P, TPQ * (c + 1), QUARTER], F32R, attn) for c in range(NQ)]
        negmax = sb("negmax", [P, NS], F32, attn)
        rowsum = sb("rowsum", [P, 4, NT], F32, attn)
        rinv = sb("rinv", [P, 4, NT], F32, attn)
        rinv_wide = sb("rinv_wide", [P, NT, 2, LD], F32, attn)
        rinv_rows = sb("rinv_rows", [P, L], F32, attn)
        low_sum = sb("low_sum", [P, NQ, QUARTER], F32, attn)
        headsT = sb("headsT", [P, NPAIR, L], F32, attn)
        x1 = sb("x1", [P, NT, D], F32, attn)
        wkv2 = sb("wkv2", [P, KD, 2, LD], F32, attn)
        wkv_hi = sb("wkv_hi", [P, KD, 2, LD], F32R, attn)
        wkv_lo = sb("wkv_lo", [P, KD, 2, LD], F32R, attn)
        wr = sb("wr", [P, KD, E], F32, attn)
        logit = sb("logit", [P, NT, E], F32, attn)
        work_a = sb("work_a", [P, NT, E], F32, attn)
        work_b = sb("work_b", [P, NT, E], F32, attn)
        onehot = sb("onehot", [P, NT, E], BF16, attn)
        earlier = sb("earlier", [P, NT, E], BF16, attn)
        in_tiles = sb("in_tiles", [P, E], F32, attn)
        rt = sb("rt", [P, 10, NT], F32, attn)
        send_idx = sb("send_idx", [P, NT], I32, attn)

        room = headsT[:, :, :].rearrange("p t d -> p (t d)")
        at = [0]

        def carve(cols):
            at[0] += cols
            return room[:, at[0] - cols:at[0]]

        wq_in = carve(KD * H * HD).rearrange("p (k n) -> p k n", k=KD)
        wqT = carve(NPAIR * D)
        wk_in = carve(H * HD)
        wv_in = carve(H * HD)
        wkT = carve(NPAIR * LD)
        wvT = carve(NPAIR * LD)
        wout_in = x1[:, :, :]
        ZR = 2
        zero_rows = carve(ZR * D)
        attn.close()

        tail = ExitStack()
        x1_all = sb("x1_all", [P, B * NT, D], F32, tail)
        experts = tail.enter_context(ExitStack())
        ex_x = sb("ex_x", [P, AHEAD, NB, D], F32, experts)
        ex_w = sb("ex_w", [P, AHEAD, 3, 2, D], F32, experts)
        ex_xT = sb("ex_xT", [P, 4, KD, C], F32, experts)
        ex_s = sb("ex_s", [P, 4, KF, C], F32, experts)
        ex_h = sb("ex_h", [P, 4, KF, C], F32, experts)
        ex_y = sb("ex_y", [P, 4, NB, D], F32, experts)
        experts.close()
        NL = min(8, B * NT // 4)
        LAST = B * NT // (2 * NL)
        half_gate = sb("half_gate", [P, B * NT], F32, tail)
        last_y = sb("last_y", [P, 2 * NL, D], F32, tail)
        last_idx = sb("last_idx", [P, 2 * NL], I32, tail)
        shift = sb("shift", [P, 2 * NL], F32, tail)
        last_o = sb("last_o", [P, 2 * NL, D], F32, tail)
        tail.close()

        const_ready = sem("const_ready")
        w_loaded = sem("w_loaded")
        zeroed = sem("zeroed")
        ring_full = sem("ring_full")
        ring_free = [sem(f"ring_free{i}") for i in range(NRING)]
        x_loaded = sem("x_loaded")
        xres_loaded = sem("xres_loaded")
        lat_hi_done = sem("lat_hi_done")
        wkv_split = sem("wkv_split")
        stage_hi_done = sem("stage_hi_done")
        fold_staged = sem("fold_staged")
        xT_hi_done = sem("xT_hi_done")
        q_hi_done = sem("q_hi_done")
        score_full = sem("score_full")
        max_done = sem("max_done")
        exp_done = sem("exp_done")
        inverse_done = sem("inverse_done")
        probT_hi_done = sem("probT_hi_done")
        low_copied = sem("low_copied")
        dve_step = sem("dve_step")
        inverse_wide = sem("inverse_wide")
        normalised = sem("normalised")
        var_ready = sem("var_ready")
        rstd_ready = sem("rstd_ready")
        x1_ready = sem("x1_ready")
        x1_kept = sem("x1_kept")
        x1_back = sem("x1_back")
        logit_ready = sem("logit_ready")
        gate_exp = sem("gate_exp")
        onehot_ready = sem("onehot_ready")
        routed = sem("routed")
        send_ready = sem("send_ready")
        sent = sem("sent")
        ex_loaded = [sem(f"ex_loaded{i}") for i in range(AHEAD)]
        ex_t_full = sem("ex_t_full")
        ex_t_ready = sem("ex_t_ready")
        ex_g_full = sem("ex_g_full")
        ex_s_ready = sem("ex_s_ready")
        ex_h_ready = [sem(f"ex_h_ready{f}") for f in range(KF)]
        ex_y_full = sem("ex_y_full")
        ex_y_free = [sem(f"ex_y_free{i}") for i in range(2)]
        ex_stored = [sem(f"ex_stored{i}") for i in range(4)]
        idx_ready = sem("idx_ready")
        fetched = [sem(f"fetched{i}") for i in range(2)]
        gates_ready = sem("gates_ready")
        shift_ready = sem("shift_ready")
        last_ready = [sem(f"last_ready{i}") for i in range(2)]
        out_stored = [sem(f"out_stored{i}") for i in range(2)]

        PRIMED = 1
        primed = [normalised, x1_kept, ex_t_ready, *ex_h_ready, *ex_y_free, *ex_stored,
                  *last_ready, *out_stored]

        def numbered(uses):
            assert len(uses) % NRING == 0, len(uses)
            return {u: i for i, u in enumerate(uses)}

        SUMS_LAG = 3
        last_of = {c: max(k for k, i in enumerate(ORDER) if i // TPQ == c) for c in range(NQ)}
        SUMS_AT = {NT * h + k + SUMS_LAG: (h, c) for h in range(4) for c, k in last_of.items()}
        SUMS_LATE = [SUMS_AT[s] for s in sorted(SUMS_AT) if s >= NS]
        SUMS_ORDER = {SUMS_AT[s]: n for n, s in enumerate(sorted(SUMS_AT))}
        Q_AT = {1: (1, 0), 3: (1, 1), 17: (0, 0), 19: (0, 1)}
        NORM_STEP = 23
        probT_uses = lambda s: [("probT", s, c) for c, _ in chunks(STEPS[s][1])]
        setup_uses = ([("wqT", c) for c in range(4)] + [("wkT", 0), ("wvT", 0)]
                      + [("A", h, kd) for h in range(2) for kd in range(KD)]
                      + [("V", h, c) for h in range(2) for c in range(4)])
        start_uses = [("xT", c) for c in range(4)] + [("lat", 0), ("lat", 1)]
        lat_keys_uses = [("lat_keys", 0), ("lat_keys", 1)]
        FIRST = numbered(setup_uses + start_uses + lat_keys_uses + [("q", 0, 0), ("q", 0, 1)])
        TURN = numbered(start_uses + [("proj", 0)] + lat_keys_uses + [("proj", i) for i in range(1, NT)] + [("x1T", 0, kd) for kd in range(KD)]
                        + [("q", 0, 0)] + [("x1T", 1, kd) for kd in range(KD)] + [("logits", 0), ("q", 0, 1), ("pos", 0)])
        loop_uses = []
        for s in range(NS):
            if s >= 1:
                loop_uses += probT_uses(s - 1)
            if s in SUMS_AT:
                loop_uses += [("sums", *SUMS_AT[s])]
            if s in Q_AT:
                loop_uses += [("q", *Q_AT[s])]
            if s == NORM_STEP:
                loop_uses += [("rinv", 0, 0), ("rinv", 0, 1)]
        loop_uses += probT_uses(NS - 1) + [("sums", *SUMS_LATE[0]), ("rinv", 1, 0), ("rinv", 1, 1)]
        loop_uses += [("sums", *sums) for sums in SUMS_LATE[1:]]
        LOOP = numbered(loop_uses)
        PROBT_ORDER = {u: i for i, u in enumerate(u for u in loop_uses if u[0] == "probT")}
        N_CHUNKS = len(PROBT_ORDER)
        BATCH_USES = G * len(LOOP) + len(TURN)

        def ring_bases(b):
            loops = len(FIRST) + b * BATCH_USES
            return loops, loops + G * len(LOOP)

        def ring_rounds(b):
            loops = len(FIRST) // NRING + b * (BATCH_USES // NRING)
            return loops, loops + G * len(LOOP) // NRING

        END_STEPS = NT + 16

        def y_use(u, n):
            return (u * NB + n) % 2, (u * NB + n) // 2

        SCORED = G * NS + 2

        def transposed(probsT, s, c, n):
            quarter, t = divmod(STEPS[s][1], TPQ)
            return probsT[quarter][:, HPB * c:HPB * c + n, t * P:(t + 1) * P]

        block = ctx.enter_context(nc.Block())

        def wait_alone(eng, sem, value):
            eng.compute_val(value)
            eng.wait_ge(const_ready, 15)
            eng.wait_ge(sem, value)

        @block.sync
        def _(sp):
            for s in primed:
                sp.sem_inc(s, PRIMED)
            sp.dma_start(wq_in, Wq.rearrange("(k p) h e -> p k (h e)", p=P)).then_inc(w_loaded, 16)
            sp.dma_start(wk_in[0:LD, :], Wk_up.rearrange("c h e -> c (h e)")).then_inc(w_loaded, 16)
            sp.dma_start(wv_in[0:LD, :], Wv_up.rearrange("c h e -> c (h e)")).then_inc(w_loaded, 16)
            sp.dma_start(wout_in, Wout.rearrange("(j h) e o -> (h e) j o", h=2)).then_inc(w_loaded, 16)
            sp.dma_start(wkv2[:, :, 0, :], Wkv.rearrange("(k p) c -> p k c", p=P)).then_inc(w_loaded, 16)
            sp.dma_start(wkv2[:, :, 1, :], Wkv.rearrange("(k p) c -> p k c", p=P)).then_inc(w_loaded, 16)
            sp.dma_start(wr[:, :, :], w_router.rearrange("(k p) e -> p k e", p=P)).then_inc(w_loaded, 16)
            sp.wait_ge(const_ready, 1)
            zero_view = slots_x.rearrange("(n r p) d -> n p r d", r=ZR, p=P)
            for n in range(zero_view.shape[0]):
                sp.dma_start(zero_view[n], zero_rows.rearrange("p (r d) -> p r d", r=ZR)).then_inc(zeroed, 16)
            sp.dma_start(x_in[:, :, :], x_tiles[0]).then_inc(x_loaded, 16)
            sp.dma_start(x_res[:, :, :], x_tiles[0]).then_inc(xres_loaded, 16)
            with sp.Fori(0, B - 1) as b:
                sp.wait_ge(ring_full, ring_bases(b)[0])
                sp.dma_start(x_in[:, :, :], x_tiles[bass.ds(b + 1, 1)].rearrange("b p t d -> p (b t) d")
                             ).then_inc(x_loaded, 16)
                sp.wait_ge(x1_ready, (b + 1) * 2)
                sp.dma_start(x_res[:, :, :], x_tiles[bass.ds(b + 1, 1)].rearrange("b p t d -> p (b t) d")
                             ).then_inc(xres_loaded, 16)
                sp.dma_start(x1_tiles[bass.ds(b, 1)].rearrange("b p t d -> p (b t) d"), x1[:, :, :]
                             ).then_inc(x1_kept, 16)
            sp.wait_ge(ring_full, len(FIRST) + (B - 1) * BATCH_USES)
            sp.dma_start(x_in[:, :, :], x_tiles[0]).then_inc(x_loaded, 16)
            sp.wait_ge(x1_ready, B * 2)
            sp.dma_start(x1_tiles[B - 1], x1[:, :, :]).then_inc(x1_kept, 16)
            sp.wait_ge(sent, 16 * NT * B)
            sp.wait_ge(fold_staged, 2 + B * (2 * G + 2))
            sp.wait_ge(routed, B)
            sp.wait_ge(exp_done, B * SCORED + 2)
            sp.wait_ge(x1_kept, 16 * B + PRIMED)

            def load_expert(g, i):
                e = g * AHEAD + i
                for m, w in enumerate((w_gate, w_up, w_down)):
                    sp.dma_start(ex_w[:, i, m], w[bass.ds(e, 1)].rearrange("e (k p) f -> p (e k) f", p=P)
                                 ).then_inc(ex_loaded[i], 16)
                rows = slots_x.rearrange("(e c) d -> e c d", c=C)[bass.ds(e, 1)]
                for n, (r0, nr) in enumerate(BLOCKS):
                    sp.dma_start(ex_x[0:nr, i, n, :], rows[:, r0:r0 + nr, :].rearrange("e p d -> p (e d)")
                                 ).then_inc(ex_loaded[i], 16)

            for i in range(AHEAD):
                load_expert(0, i)
            for b in range(B):
                sp.dma_start(x1_all[:, b * NT:(b + 1) * NT, :], x1_tiles[b]).then_inc(x1_back, 16)
            with sp.Fori(0, E // AHEAD - 1) as g:
                for c in range(0, AHEAD, 2):
                    for i in range(2):
                        sp.wait_ge(ex_y_free[i], g * (AHEAD // 2 * NB) + ((c // 2 + 1) * NB + PRIMED))
                    for u in range(2):
                        load_expert(g + 1, c + u)
            with sp.Fori(0, LAST) as g:
                for u in range(2):
                    sp.wait_ge(last_ready[u], g + 1 + PRIMED)
                    sp.dma_start(out_tiles[bass.ds((g * 2 + u) * NL, NL)].rearrange("t p d -> p t d"),
                                 last_o[:, u * NL:(u + 1) * NL, :]).then_inc(out_stored[u], 16)
            for u in range(2):
                sp.wait_ge(out_stored[u], 16 * LAST + PRIMED)

        @block.gpsimd
        def _(pool):
            nc.gpsimd.memset(zero_rows, 0.0).then_inc(const_ready, 1)
            nc.gpsimd.memset(fold_q[:, :, NPAIR * P:], 0.0).then_inc(const_ready, 1)
            nc.gpsimd.memset(low_sum[:, :, :], 0.0).then_inc(const_ready, 1)
            nc.gpsimd.memset(earlier[:, :, :], 0.0).then_inc(const_ready, 1)
            nc.gpsimd.memset(ident[:, :], 0.0).then_inc(const_ready, 1)
            nc.gpsimd.memset(future_bf[:, :], 0.0).then_inc(const_ready, 1)
            nc.gpsimd.memset(before_bf[:, :], 1.0).then_inc(const_ready, 1)
            nc.gpsimd.memset(ones_bf[:, :], 1.0).then_inc(const_ready, 1)
            nc.gpsimd.memset(minus_half[:, :], -0.5).then_inc(const_ready, 1)
            nc.gpsimd.iota(expert_i[:, :], [[1, E]], base=-E, channel_multiplier=0).then_inc(const_ready, 1)
            pool.wait_ge(const_ready, 10)
            nc.gpsimd.affine_select(out=ident[:, :], in_=ident[:, :], pattern=[[-1, P]], compare_op=ALU.not_equal,
                                    fill=1.0, base=0, channel_multiplier=1).then_inc(const_ready, 1)
            nc.gpsimd.affine_select(out=future_bf[:, :], in_=future_bf[:, :], pattern=[[-1, P]], compare_op=ALU.is_ge,
                                    fill=MASKED, base=0, channel_multiplier=1).then_inc(const_ready, 1)
            nc.gpsimd.affine_select(out=before_bf[:, :], in_=before_bf[:, :], pattern=[[1, P]], compare_op=ALU.is_gt,
                                    fill=0.0, base=0, channel_multiplier=-1).then_inc(const_ready, 1)
            nc.gpsimd.tensor_copy(expert_m[:, :], expert_i[:, :]).then_inc(const_ready, 1)
            pool.wait_ge(const_ready, 14)
            nc.gpsimd.tensor_copy(ident_bf[:, :], ident[:, :]).then_inc(const_ready, 1)
            for c in range(KD):
                n = FIRST[("A", 1, c)]
                pool.wait_ge(ring_free[n % NRING], n // NRING + 1)
            pool.wait_ge(w_loaded, 16 * 7)
            nc.gpsimd.tensor_copy(wkv_hi[:, :, :, :], wkv2[:, :, :, :]).then_inc(wkv_split, 1)
            pool.wait_ge(wkv_split, 1)
            nc.gpsimd.tensor_tensor(wkv_lo[:, :, :, :], wkv2[:, :, :, :], wkv_hi[:, :, :, :].bitcast(F32), ALU.subtract
                                    ).then_inc(wkv_split, 1)

            def stage(pair, count):
                w = fold_q[:, :, bass.ds(pair * P, P)]
                nc.gpsimd.tensor_copy(stage_hi[:, :, :], w).then_inc(stage_hi_done, 1)
                wait_alone(pool, stage_hi_done, count)
                nc.gpsimd.tensor_tensor(stage_lo[:, :, :], w, stage_hi[:, :, :].bitcast(F32), ALU.subtract
                                        ).then_inc(fold_staged, 1)

            stage(0, 1)
            pool.wait_ge(ring_full, len(FIRST))
            stage(1, 2)
            pool.wait_ge(zeroed, 16 * (SLOTS // (ZR * P)))
            with pool.Fori(0, B) as b:
                with pool.Fori(0, G) as g:
                    base = pool.snap(ring_bases(b)[0] + g * len(LOOP))
                    rounds = pool.snap(ring_rounds(b)[0] + g * (len(LOOP) // NRING))
                    for q in range(2):
                        wait_alone(pool, ring_full, base + LOOP[("q", 1 - q, 1)] + 1)
                        stage(2 * g + 2 + q, b * (2 * G + 2) + (g * 2 + 3 + q))
                        pair = (b * G + g) * 2 + q
                        if q == 0:
                            wait_alone(pool, inverse_done, (b * G + g) * 2 + 1)
                            for h in range(2):
                                ins = nc.gpsimd.tensor_copy(rinv_wide[:, :, h, :],
                                                            rinv[:, h, :].unsqueeze(2).to_broadcast([P, NT, LD]))
                            ins.then_inc(inverse_wide, 1)
                        uses = [("rinv", q, c) for c in range(2)] + [("sums", 2 * q + h, c) for h in range(2) for c in range(NQ)]
                        for n in {n % NRING: n for n in sorted(LOOP[use] for use in uses)}.values():
                            wait_alone(pool, ring_free[n % NRING], rounds + n // NRING + 1)
                        dst = headsT[:, bass.ds(2 * g + q, 1), :].rearrange("p a n -> p (a n)")
                        nc.gpsimd.tensor_tensor(dst, dst, rinv_rows[:, :], ALU.mult).then_inc(normalised, 1)
                wait_alone(pool, fold_staged, (b + 1) * (2 * G + 2))
                stage(0, b * (2 * G + 2) + (2 * G + 3))
                for hf in range(2):
                    tiles = slice(hf * HPB, (hf + 1) * HPB)
                    wait_alone(pool, var_ready, b * 2 + (hf + 1))
                    nc.gpsimd.tensor_tensor(rstd[:, tiles], var_eps[:, tiles], minus_half[:, tiles], ALU.pow
                                            ).then_inc(rstd_ready, 1)
                wait_alone(pool, ring_full, ring_bases(b)[1] + TURN[("q", 0, 1)] + 1)
                stage(1, b * (2 * G + 2) + (2 * G + 4))
                wait_alone(pool, send_ready, b + 1)
                for i in range(NT):
                    nc.gpsimd.indirect_dma_start(
                        out=slots_x, out_offset=bass.IndirectOffsetOnAxis(ap=send_idx[:, i:i + 1], axis=0),
                        in_=x1[:, i, :], in_offset=None, bounds_check=SLOTS - 1, oob_is_err=False).then_inc(sent, 16)
                wait_alone(pool, sent, (b + 1) * (16 * NT))
            for k in range(4):
                pool.wait_ge(ex_stored[k], 16 * NB * (E // 4) + PRIMED)
            def fetch(n, u):
                nc.gpsimd.tensor_copy(last_idx[:, u * NL:(u + 1) * NL], fetch_all[:, bass.ds(n * NL, NL)]
                                      ).then_inc(idx_ready, 1)
                wait_alone(pool, idx_ready, n + 1)
                for i in range(NL):
                    nc.gpsimd.indirect_dma_start(
                        out=last_y[:, u * NL + i, :], out_offset=None, in_=slots_y,
                        in_offset=bass.IndirectOffsetOnAxis(ap=last_idx[:, u * NL + i:u * NL + i + 1], axis=0),
                        bounds_check=SLOTS - 1, oob_is_err=False).then_inc(fetched[u], 16)

            def root(n, u):
                half_ = slice(u * NL, (u + 1) * NL)
                wait_alone(pool, var_ready, n + (2 * B + 1))
                nc.gpsimd.tensor_tensor(rstd[:, half_], var_eps[:, half_], minus_half[:, half_], ALU.pow
                                        ).then_inc(rstd_ready, 1)

            fetch(0, 0)
            with pool.Fori(0, LAST - 1) as g:
                wait_alone(pool, last_ready[1], g + PRIMED)
                fetch(g * 2 + 1, 1)
                root(g * 2, 0)
                wait_alone(pool, last_ready[0], g + 1 + PRIMED)
                fetch(g * 2 + 2, 0)
                root(g * 2 + 1, 1)
            wait_alone(pool, last_ready[1], LAST - 1 + PRIMED)
            fetch(LAST * 2 - 1, 1)
            root(LAST * 2 - 2, 0)
            root(LAST * 2 - 1, 1)

        @block.tensor
        def _(pe):
            rounds = {"first": 0}

            def ring_wait(part, uses, use):
                n = uses[use]
                pe.wait_ge(ring_free[n % NRING], rounds[part] + n // NRING)
                return ring[n % NRING]

            def evacuated(part, uses, use):
                n = uses[use]
                pe.wait_ge(ring_free[n % NRING], rounds[part] + n // NRING + 1)

            pe.wait_ge(const_ready, 15)
            pe.wait_ge(w_loaded, 16 * 7)
            for c in range(4):
                bank = ring_wait("first", FIRST, ("wqT", c))
                for k in range(4):
                    j, kd = 2 * c + k // 2, k % 2
                    mm = nc.tensor.transpose(bank[:, k * P:(k + 1) * P], wq_in[:, kd, j * P:(j + 1) * P], ident[:, :])
                mm.then_inc(ring_full, 1)
            for name, w in (("wkT", wk_in), ("wvT", wv_in)):
                bank = ring_wait("first", FIRST, (name, 0))
                for j in range(NPAIR):
                    mm = nc.tensor.transpose(bank[:, j * LD:(j + 1) * LD], w[0:LD, j * P:(j + 1) * P], ident[0:LD, 0:LD])
                mm.then_inc(ring_full, 1)
            for c in range(4):
                evacuated("first", FIRST, ("wqT", c))
            evacuated("first", FIRST, ("wkT", 0))
            evacuated("first", FIRST, ("wvT", 0))
            for h in range(2):
                rows = slice(h * HD, (h + 1) * HD)
                for kd in range(KD):
                    bank = ring_wait("first", FIRST, ("A", h, kd))
                    for j in range(NPAIR):
                        mm = nc.tensor.matmul(bank[:, j * LD:(j + 1) * LD],
                                              wqT[rows, j * D + kd * P:j * D + (kd + 1) * P],
                                              wkT[rows, j * LD:(j + 1) * LD], start=True, stop=True)
                    mm.then_inc(ring_full, 1)
            for h in range(2):
                rows = slice(h * HD, (h + 1) * HD)
                for c in range(4):
                    bank = ring_wait("first", FIRST, ("V", h, c))
                    for j in (2 * c, 2 * c + 1):
                        mm = nc.tensor.matmul(bank[rows, (j % 2) * D:(j % 2 + 1) * D], wvT[rows, j * LD:(j + 1) * LD],
                                              wout_in[rows, j, :], start=True, stop=True)
                    mm.then_inc(ring_full, 1)
            for c in range(4):
                evacuated("first", FIRST, ("V", 1, c))

            def product(bank, w_hi, w_lo, hf):
                passes = [(w, x, kd) for w, x in ((w_hi, xT_hi), (w_lo, xT_hi), (w_hi, xT_lo)) for kd in range(KD)]
                for n, (w, x, kd) in enumerate(passes):
                    mm = nc.tensor.matmul(bank[:, :], w[:, kd] if len(w.shape) == 3 else w[:, kd].rearrange("p a c -> p (a c)"),
                                          x[:, kd, hf * BANK:(hf + 1) * BANK], start=(n == 0), stop=(n == len(passes) - 1))
                return mm

            def project_q(base, uses, *use):
                bank = ring_wait(base, uses, ("q", *use))
                hf = use[-1]
                mm = product(bank, stage_hi, stage_lo, hf)
                mm.then_inc(ring_full, 1)

            def scores(s, scored0):
                h, i = STEPS[s % NS]
                if s >= 2:
                    pe.wait_ge(exp_done, scored0 + s - 1)
                keys = (i + 1) * P
                q = q_hl[:, h // 2, h % 2, i * P:(i + 1) * P]
                for k0 in range(0, keys, BANK):
                    k1 = min(keys, k0 + BANK)
                    dst = score_ps[s % 2]
                    nc.tensor.matmul(dst[:, k0:k1], q, lat_hi[:, k0:k1], start=True, stop=False)
                    if k1 == keys:
                        nc.tensor.matmul(dst[:, keys - P:keys], ident_bf[:, :], future_bf[:, :],
                                         start=False, stop=False)
                    mm = nc.tensor.matmul(dst[:, k0:k1], q, lat_lo[:, k0:k1], start=False, stop=True)
                mm.then_inc(score_full, 1)

            def transpose_x(base, uses):
                for c in range(4):
                    bank = ring_wait(base, uses, ("xT", c))
                    kd, t0 = c // 2, HPB * (c % 2)
                    for k in range(HPB):
                        mm = nc.tensor.transpose(bank[:, k * P:(k + 1) * P], x_in[:, t0 + k, kd * P:(kd + 1) * P],
                                                 ident[:, :])
                    mm.then_inc(ring_full, 1)

            def make_latents(base, uses):
                for hf in range(2):
                    evacuated(base, uses, ("xT", hf))
                    evacuated(base, uses, ("xT", 2 + hf))
                    bank = ring_wait(base, uses, ("lat", hf))
                    mm = product(bank, wkv_hi, wkv_lo, hf)
                    mm.then_inc(ring_full, 1)

            def transpose_latents(base, uses):
                for hf in range(2):
                    evacuated(base, uses, ("lat", hf))
                    bank = ring_wait(base, uses, ("lat_keys", hf))
                    for k in range(HPB):
                        i = hf * HPB + k
                        nc.tensor.transpose(bank[:, k * P:(k + 1) * P], lat_hi[:, i * P:(i + 1) * P].bitcast(F32), ident[:, :])
                        mm = nc.tensor.transpose(bank[:, k * P + LD:(k + 1) * P], lat_lo[0:LD, i * P:(i + 1) * P].bitcast(F32),
                                                 ident[0:LD, 0:LD])
                    mm.then_inc(ring_full, 1)

            pe.wait_ge(x_loaded, 16)
            transpose_x("first", FIRST)
            pe.wait_ge(wkv_split, 2)
            make_latents("first", FIRST)
            transpose_latents("first", FIRST)
            pe.wait_ge(fold_staged, 1)
            for hf in range(2):
                project_q("first", FIRST, 0, hf)
            for use in [("lat", 1), ("lat_keys", 1), ("q", 0, 0), ("q", 0, 1)]:
                evacuated("first", FIRST, use)
            for s in range(2):
                scores(s, None)

            with pe.Fori(0, B) as b:
                with pe.Fori(0, G) as g:
                    rounds["loop"] = pe.snap(ring_rounds(b)[0] + g * (len(LOOP) // NRING))
                    pairs2 = b * G + g
                    scored0 = pe.snap(b * SCORED + g * NS)

                    def transpose_probs(s):
                        h, i = STEPS[s]
                        pe.wait_ge(exp_done, scored0 + s + 1)
                        for c, n in chunks(i):
                            bank = ring_wait("loop", LOOP, ("probT", s, c))
                            for k in range(n):
                                j = HPB * c + k
                                mm = nc.tensor.transpose(bank[:, k * P:(k + 1) * P],
                                                         probs[:, s % NPROBS, j * P:(j + 1) * P], ident[:, :])
                            mm.then_inc(ring_full, 1)

                    def spread_inverse(q):
                        pe.wait_ge(inverse_wide, pairs2 * 2 + q + 1)
                        for c in range(2):
                            bank = ring_wait("loop", LOOP, ("rinv", q, c))
                            for k in range(HPB):
                                i = HPB * c + k
                                mm = nc.tensor.transpose(bank[:, k * P:(k + 1) * P],
                                                         rinv_wide[:, i].rearrange("p a c -> p (a c)"),
                                                         ident[:, :])
                            mm.then_inc(ring_full, 1)

                    def times_latents(h, c):
                        last_use = {}
                        for s in range(h * NT, (h + 1) * NT):
                            if STEPS[s][1] // TPQ == c:
                                last_use.update({LOOP[use] % NRING: use for use in probT_uses(s)})
                        for n, use in last_use.items():
                            if n != LOOP[("sums", h, c)] % NRING:
                                evacuated("loop", LOOP, use)
                        bank = ring_wait("loop", LOOP, ("sums", h, c))
                        blocks = TPQ * (c + 1)
                        for j in range(blocks):
                            q0 = max(0, j - TPQ * c) * P
                            for part in (probsT_hi, probsT_lo):
                                mm = nc.tensor.matmul(bank[:, q0:QUARTER], lat_keys[:, j].rearrange("p a c -> p (a c)"),
                                                      part[c][:, j, q0:QUARTER], start=(j == 0 and part is probsT_hi),
                                                      stop=(j == blocks - 1 and part is probsT_lo))
                        mm.then_inc(ring_full, 1)

                    for s in range(NS):
                        scores(s + 2, scored0)
                        if s >= 1:
                            transpose_probs(s - 1)
                        if s in SUMS_AT:
                            times_latents(*SUMS_AT[s])
                        if s in Q_AT:
                            pair, hf = Q_AT[s]
                            pe.wait_ge(fold_staged, b * (2 * G + 2) + (g * 2 + 3 - pair))
                            project_q("loop", LOOP, pair, hf)
                        if s == NORM_STEP:
                            spread_inverse(0)
                    transpose_probs(NS - 1)
                    times_latents(*SUMS_LATE[0])
                    spread_inverse(1)
                    for sums in SUMS_LATE[1:]:
                        times_latents(*sums)

                rounds["turn"] = pe.snap(ring_rounds(b)[1])
                pe.wait_ge(x_loaded, (b + 2) * 16)
                transpose_x("turn", TURN)
                make_latents("turn", TURN)
                pe.wait_ge(normalised, (b + 1) * NPAIR + PRIMED)
                for i in range(NT):
                    if i == 1:
                        transpose_latents("turn", TURN)
                    bank = ring_wait("turn", TURN, ("proj", i))
                    for j in range(NPAIR):
                        mm = nc.tensor.matmul(bank[:, 0:D], headsT[:, j, i * P:(i + 1) * P], fold_v[:, j, :],
                                              start=(j == 0), stop=(j == NPAIR - 1))
                    mm.then_inc(ring_full, 1)

                def transpose_x1(hf):
                    pe.wait_ge(x1_ready, b * 2 + (hf + 1))
                    for kd in range(KD):
                        bank = ring_wait("turn", TURN, ("x1T", hf, kd))
                        for k in range(HPB):
                            mm = nc.tensor.transpose(bank[:, k * P:(k + 1) * P],
                                                     x1[:, hf * HPB + k, kd * P:(kd + 1) * P], ident[:, :])
                        mm.then_inc(ring_full, 1)

                transpose_x1(0)
                pe.wait_ge(fold_staged, b * (2 * G + 2) + (2 * G + 3))
                project_q("turn", TURN, 0, 0)
                transpose_x1(1)
                for kd in range(KD):
                    evacuated("turn", TURN, ("x1T", 1, kd))
                bank = ring_wait("turn", TURN, ("logits", 0))
                for i in range(NT):
                    for kd in range(KD):
                        mm = nc.tensor.matmul(bank[:, i * E:(i + 1) * E], x1T[:, kd, i * P:(i + 1) * P],
                                              wr[:, kd, :], start=(kd == 0), stop=(kd == KD - 1))
                mm.then_inc(ring_full, 1)
                project_q("turn", TURN, 0, 1)
                bank = ring_wait("turn", TURN, ("pos", 0))
                pe.wait_ge(onehot_ready, b + 1)
                nc.tensor.matmul(bank[:, 0:NT * E], before_bf[:, :], onehot[:, :, :].rearrange("p t e -> p (t e)"),
                                 start=True, stop=False)
                for d in range(1, NT):
                    nc.tensor.matmul(bank[:, d * E:NT * E], ones_bf[:, :],
                                     onehot[:, 0:NT - d, :].rearrange("p t e -> p (t e)"), start=False, stop=False)
                nc.tensor.matmul(bank[:, 0:NT * E], ones_bf[:, :], earlier[:, :, :].rearrange("p t e -> p (t e)"),
                                 start=False, stop=True).then_inc(ring_full, 1)
                evacuated("turn", TURN, ("q", 0, 1))
                for s in range(2):
                    scores(s, None)

            pe.wait_ge(routed, B)
            pe.wait_ge(exp_done, B * SCORED + 2)
            def transpose_rows(g, i):
                k = i % AHEAD
                pe.wait_ge(ex_loaded[k], (g + (i // AHEAD + 1)) * (16 * (3 + NB)))
                pe.wait_ge(ex_t_ready, g * AHEAD + (i + PRIMED))
                for kd in range(KD):
                    for n, (r0, nr) in enumerate(BLOCKS):
                        mm = nc.tensor.transpose(ring[kd][:, r0:r0 + nr], ex_x[0:nr, k, n, kd * P:(kd + 1) * P],
                                                 ident[0:nr, 0:nr])
                mm.then_inc(ex_t_full, 1)

            def gate_and_up(g, i):
                pe.wait_ge(ex_t_ready, g * AHEAD + (i + 1 + PRIMED))
                for f in range(KF):
                    pe.wait_ge(ex_h_ready[f], g * AHEAD + (i + PRIMED))
                    for m in range(2):
                        for kd in range(KD):
                            mm = nc.tensor.matmul(score_ps[f][:, m * BANK:m * BANK + C],
                                                  ex_w[:, i, m, kd, f * P:(f + 1) * P], ex_xT[:, i % 4, kd, :],
                                                  start=(kd == 0), stop=(kd == KD - 1))
                    mm.then_inc(ex_g_full, 1)

            def down(g, i):
                for f in range(KF):
                    pe.wait_ge(ex_h_ready[f], g * AHEAD + (i + 1 + PRIMED))
                for n, (r0, nr) in enumerate(BLOCKS):
                    bank, uses = y_use(i % 2, n)
                    pe.wait_ge(ex_y_free[bank], g * (AHEAD // 2 * NB) + (i // 2 * NB + uses + PRIMED))
                    for f in range(KF):
                        mm = nc.tensor.matmul(ring[2 + bank][0:nr, 0:D], ex_h[:, i % 4, f, r0:r0 + nr],
                                              ex_w[:, i, 2, f, :], start=(f == 0), stop=(f == KF - 1))
                    mm.then_inc(ex_y_full, 1)

            def couples(g, last):
                for i in range(0, AHEAD, 2):
                    for u in range(2):
                        gate_and_up(g, i + u)
                        if not (last and i + u + 2 >= AHEAD):
                            transpose_rows(g, i + u + 2)
                    for u in range(2):
                        down(g, i + u)

            for i in range(2):
                transpose_rows(0, i)
            with pe.Fori(0, E // AHEAD - 1) as g:
                couples(g, last=False)
            couples(E // AHEAD - 1, last=True)

        @block.scalar
        def _(act):
            def full(base, uses, use):
                n = uses[use]
                act.wait_ge(ring_full, base + n + 1)
                return ring[n % NRING], ring_free[n % NRING]

            for name, dst in (("wkT", wkT), ("wvT", wvT)):
                bank, done = full(0, FIRST, (name, 0))
                nc.scalar.copy(dst, bank[:, :]).then_inc(done, 1)
            for h in range(2):
                rows = slice(h * HD, (h + 1) * HD)
                for c in range(4):
                    bank, done = full(0, FIRST, ("V", h, c))
                    nc.scalar.copy(fold_v[rows, 2 * c:2 * c + 2, :].rearrange("p j n -> p (j n)"), bank[rows, :]
                                   ).then_inc(done, 1)

            def split_hi(base, uses, pair, *use):
                bank, _ = full(base, uses, ("q", *use))
                cols = slice(use[-1] * BANK, (use[-1] + 1) * BANK)
                nc.scalar.copy(q_hl[0:64, pair, 0, cols], bank[0:64, :])
                nc.scalar.copy(q_hl[64:128, pair, 1, cols], bank[64:128, :]).then_inc(q_hi_done, 1)

            def high_of_start(base, uses):
                for c in range(4):
                    bank, _ = full(base, uses, ("xT", c))
                    nc.scalar.copy(xT_hi[:, c // 2, (c % 2) * BANK:(c % 2 + 1) * BANK], bank[:, :]).then_inc(xT_hi_done, 1)
                for hf in range(2):
                    bank, _ = full(base, uses, ("lat", hf))
                    nc.scalar.copy(lat_hi[:, hf * BANK:(hf + 1) * BANK], bank[:, :]).then_inc(lat_hi_done, 1)
                for hf in range(2):
                    bank, done = full(base, uses, ("lat_keys", hf))
                    nc.scalar.copy(lat_keys[:, hf * HPB:(hf + 1) * HPB, :, :].rearrange("p t a c -> p (t a c)"), bank[:, :]
                                   ).then_inc(done, 1)

            def exponentials(s, scored0, base):
                keys = (STEPS[s % NS][1] + 1) * P
                act.wait_ge(max_done, scored0 + s + 1)
                if s >= NPROBS:
                    act.wait_ge(ring_full, base + LOOP[probT_uses(s - NPROBS)[-1]] + 1)
                nc.scalar.activation(probs[:, s % NPROBS, 0:keys], score_ps[s % 2][:, 0:keys], ACT.Exp,
                                     bias=negmax[:, s % NS:s % NS + 1],
                                     accum_out=rowsum[:, STEPS[s % NS][0], STEPS[s % NS][1]:STEPS[s % NS][1] + 1]
                                     ).then_inc(exp_done, 1)

            high_of_start(0, FIRST)
            for hf in range(2):
                split_hi(0, FIRST, 0, 0, hf)
            for s in range(2):
                exponentials(s, 0, None)

            with act.Fori(0, B) as b:
                loops, turn = ring_bases(b)
                with act.Fori(0, G) as g:
                    base = act.snap(loops + g * len(LOOP))
                    scored0 = act.snap(b * SCORED + g * NS)

                    def copy_low(h, c):
                        bank, _ = full(base, LOOP, ("sums", h, c))
                        nc.scalar.copy(low_sum[0:LD, c, :], bank[LD:2 * LD, 0:QUARTER]).then_inc(low_copied, 1)

                    def copy_inverse(q):
                        act.wait_ge(normalised, (b * G + g) * 2 + (q + PRIMED))
                        for c in range(2):
                            bank, done = full(base, LOOP, ("rinv", q, c))
                            nc.scalar.copy(rinv_rows[:, c * BANK:(c + 1) * BANK], bank[:, :]).then_inc(done, 1)

                    def high_parts(s):
                        h, i = STEPS[s]
                        if h >= 1:
                            act.wait_ge(ring_full, base + LOOP[("sums", h - 1, i // TPQ)] + 1)
                        for c, n in chunks(i):
                            bank, _ = full(base, LOOP, ("probT", s, c))
                            nc.scalar.copy(transposed(probsT_hi, s, c, n),
                                           bank[:, 0:n * P].rearrange("p (k q) -> p k q", k=n)).then_inc(probT_hi_done, 1)

                    for s in range(NS + 2):
                        if s >= 2:
                            exponentials(s, scored0, base)
                        if s >= HI_LAG:
                            high_parts(s - HI_LAG)
                        if s - 1 in Q_AT:
                            split_hi(base, LOOP, Q_AT[s - 1][0], *Q_AT[s - 1])
                        if s - 1 == NORM_STEP:
                            copy_inverse(0)
                        if s - 1 < NS and s - 1 in SUMS_AT:
                            copy_low(*SUMS_AT[s - 1])
                    copy_low(*SUMS_LATE[0])
                    copy_inverse(1)
                    for sums in SUMS_LATE[1:]:
                        copy_low(*sums)

                turn = act.snap(turn)
                high_of_start(turn, TURN)

                def copy_x1T(hf):
                    for kd in range(KD):
                        bank, done = full(turn, TURN, ("x1T", hf, kd))
                        nc.scalar.copy(x1T[:, kd, hf * BANK:(hf + 1) * BANK], bank[:, :]).then_inc(done, 1)

                copy_x1T(0)
                split_hi(turn, TURN, 0, 0, 0)
                copy_x1T(1)
                split_hi(turn, TURN, 0, 0, 1)
                act.wait_ge(logit_ready, b + 1)
                nc.scalar.activation(work_b[:, :, :], work_a[:, :, :], ACT.Exp).then_inc(gate_exp, 1)
                for s in range(2):
                    exponentials(s, b * SCORED + SCORED, None)

            with act.Fori(0, E // AHEAD) as g:
                for i in range(0, AHEAD, 2):
                    for k in (i, i + 1):
                        for f in range(KF):
                            act.wait_ge(ex_g_full, g * (AHEAD * KF) + (k * KF + f + 1))
                            nc.scalar.activation(ex_s[:, k % 4, f, :], score_ps[f][:, 0:C], ACT.Silu).then_inc(ex_s_ready, 1)
                    for u, k in enumerate((i, i + 1)):
                        for n in range(max(0, NB - 2), NB):
                            bank, uses = y_use(u, n)
                            act.wait_ge(ex_y_free[bank], g * (AHEAD // 2 * NB) + (i // 2 * NB + uses + 1 + PRIMED))
                        rows = slots_y.rearrange("(e c) d -> e c d", c=C)[bass.ds(g * AHEAD + k, 1)]
                        for n, (r0, nr) in enumerate(BLOCKS):
                            act.dma_start(rows[:, r0:r0 + nr, :].rearrange("e p d -> p (e d)"), ex_y[0:nr, k % 4, n, :]
                                          ).then_inc(ex_stored[k % 4], 16)

            with act.Fori(0, LAST) as g:
                for u in range(2):
                    act.wait_ge(shift_ready, g * 2 + (u + 1))
                    act.wait_ge(out_stored[u], g * 16 + PRIMED)
                    for i in range(NL):
                        k = u * NL + i
                        last = nc.scalar.activation(last_o[:, k, :], last_y[:, k, :], ACT.Identity,
                                                    bias=shift[:, k:k + 1], scale=rstd[:, k:k + 1])
                    last.then_inc(last_ready[u], 1)

        @block.vector
        def _(dve):
            def full(base, uses, use):
                n = uses[use]
                dve.wait_ge(ring_full, base + n + 1)
                return ring[n % NRING], ring_free[n % NRING]

            steps = [0, 0]

            def step(ins):
                steps[1] += 1
                ins.then_inc(dve_step, 1)

            def settle(alone=False):
                if alone:
                    wait_alone(dve, dve_step, steps[0] + steps[1])
                else:
                    dve.wait_ge(dve_step, steps[0] + steps[1])

            for c in range(4):
                bank, done = full(0, FIRST, ("wqT", c))
                nc.vector.tensor_copy(wqT[:, c * BANK:(c + 1) * BANK], bank[:, :]).then_inc(done, 1)
            for h in range(2):
                for kd in range(KD):
                    bank, done = full(0, FIRST, ("A", h, kd))
                    dst = fold_q[:, kd, 0:NPAIR * P].rearrange("p (j h c) -> p j h c", h=2, c=LD)[:, :, h, :]
                    nc.vector.tensor_scalar(dst, bank[:, :].rearrange("p (j c) -> p j c", c=LD),
                                            float(HD) ** -0.5, None, ALU.mult).then_inc(done, 1)

            def split_lo(base, uses, pair, count, *use):
                dve.wait_ge(q_hi_done, count + use[-1] + 1)
                bank, done = full(base, uses, ("q", *use))
                cols = slice(use[-1] * BANK, (use[-1] + 1) * BANK)
                nc.vector.tensor_tensor(q_hl[64:128, pair, 0, cols], bank[0:64, :], q_hl[0:64, pair, 0, cols].bitcast(F32),
                                        ALU.subtract)
                nc.vector.tensor_tensor(q_hl[0:64, pair, 1, cols], bank[64:128, :], q_hl[64:128, pair, 1, cols].bitcast(F32),
                                        ALU.subtract).then_inc(done, 1)

            def row_max(s, scored0):
                keys = (STEPS[s % NS][1] + 1) * P
                dve.wait_ge(score_full, scored0 + s + 1)
                nc.vector.tensor_reduce(negmax[:, s % NS:s % NS + 1], score_ps[s % 2][:, 0:keys], AX.X, ALU.max,
                                        negate=True).then_inc(max_done, 1)

            dve.wait_ge(zeroed, 16 * (SLOTS // (ZR * P)))
            def low_of_start(base, uses, n):
                for c in range(4):
                    dve.wait_ge(xT_hi_done, n * 4 + (c + 1))
                    bank, done = full(base, uses, ("xT", c))
                    cols = slice((c % 2) * BANK, (c % 2 + 1) * BANK)
                    nc.vector.tensor_tensor(xT_lo[:, c // 2, cols], bank[:, :], xT_hi[:, c // 2, cols].bitcast(F32),
                                            ALU.subtract).then_inc(done, 1)
                for hf in range(2):
                    dve.wait_ge(lat_hi_done, n * 2 + (hf + 1))
                    bank, done = full(base, uses, ("lat", hf))
                    cols = slice(hf * BANK, (hf + 1) * BANK)
                    nc.vector.tensor_tensor(lat_lo[:, cols], bank[:, :], lat_hi[:, cols].bitcast(F32), ALU.subtract
                                            ).then_inc(done, 1)

            low_of_start(0, FIRST, 0)
            for hf in range(2):
                split_lo(0, FIRST, 0, 0, 0, hf)
            for s in range(2):
                row_max(s, 0)

            with dve.Fori(0, B) as b:
                loops, turn = ring_bases(b)
                with dve.Fori(0, G) as g:
                    base = dve.snap(loops + g * len(LOOP))
                    scored0 = dve.snap(b * SCORED + g * NS)
                    chunk0 = dve.snap((b * G + g) * N_CHUNKS)

                    def low_parts(s):
                        for c, n in chunks(STEPS[s][1]):
                            dve.wait_ge(probT_hi_done, chunk0 + PROBT_ORDER[("probT", s, c)] + 1)
                            bank, done = full(base, LOOP, ("probT", s, c))
                            nc.vector.tensor_tensor(transposed(probsT_lo, s, c, n),
                                                    bank[:, 0:n * P].rearrange("p (k q) -> p k q", k=n),
                                                    transposed(probsT_hi, s, c, n).bitcast(F32), ALU.subtract
                                                    ).then_inc(done, 1)

                    def add_sums(h, c):
                        dve.wait_ge(low_copied, (b * G + g) * (4 * NQ) + (SUMS_ORDER[(h, c)] + 1))
                        bank, done = full(base, LOOP, ("sums", h, c))
                        pair = bass.ds(2 * g + h // 2, 1)
                        cols = slice(c * QUARTER, (c + 1) * QUARTER)
                        nc.vector.tensor_tensor(
                            headsT[(h % 2) * LD:(h % 2 + 1) * LD, pair, cols].rearrange("p a n -> p (a n)"),
                            bank[0:LD, 0:QUARTER], low_sum[0:LD, c, :], ALU.add).then_inc(done, 1)

                    for s in range(NS + LO_LAG):
                        if 2 <= s < NS + 2:
                            row_max(s, scored0)
                        if s in (NS // 2, NS):
                            q = 2 * s // NS - 1
                            dve.wait_ge(exp_done, scored0 + s)
                            nc.vector.reciprocal(rinv[:, 2 * q:2 * q + 2, :], rowsum[:, 2 * q:2 * q + 2, :]
                                                 ).then_inc(inverse_done, 1)
                            if q == 1:
                                dve.wait_ge(inverse_done, (b * G + g) * 2 + 2)
                                for h in range(2):
                                    ins = nc.vector.tensor_copy(rinv_wide[:, :, h, :],
                                                                rinv[:, 2 + h, :].unsqueeze(2).to_broadcast([P, NT, LD]))
                                ins.then_inc(inverse_wide, 1)
                        if s >= LO_LAG:
                            low_parts(s - LO_LAG)
                        if s - 2 < NS and s - 2 in SUMS_AT:
                            add_sums(*SUMS_AT[s - 2])
                        if s - 2 in Q_AT:
                            pair, hf = Q_AT[s - 2]
                            split_lo(base, LOOP, pair, b * (4 * G + 2) + (4 * g + 4 - 2 * pair), pair, hf)
                    for sums in SUMS_LATE:
                        add_sums(*sums)

                turn = dve.snap(turn)
                turn_rounds = dve.snap(ring_rounds(b)[1])
                steps[0] = dve.snap(b * END_STEPS)
                steps[1] = 0

                def own(use):
                    n = TURN[use]
                    dve.wait_ge(ring_free[n % NRING], turn_rounds + (n // NRING + 1))

                low_of_start(turn, TURN, b + 1)
                dve.wait_ge(xres_loaded, (b + 1) * 16)
                dve.wait_ge(x1_kept, b * 16 + PRIMED)

                def add_and_count(i, h0):
                    bank, done = full(turn, TURN, ("proj", i))
                    nc.vector.tensor_tensor(x1[:, i, :], bank[:, 0:D], x_res[:, i, :], ALU.add).then_inc(done, 1)
                    if i > h0:
                        statistics(i - 1)

                def statistics(i):
                    own(("proj", i))
                    step(nc.vector.bn_stats(stat6[:, i, :], x1[:, i, :]))

                def variance(hf):
                    settle(alone=True)
                    for i in range(hf * HPB, (hf + 1) * HPB):
                        last = nc.vector.bn_aggr(mean_var[:, i, :], stat6[:, i, :])
                    step(last)
                    settle()
                    nc.vector.tensor_scalar(var_eps[:, hf * HPB:(hf + 1) * HPB], mean_var[:, hf * HPB:(hf + 1) * HPB, 1],
                                            EPS, None, ALU.add).then_inc(var_ready, 1)

                def normalise(hf):
                    dve.wait_ge(rstd_ready, b * 2 + (hf + 1))
                    for i in range(hf * HPB, (hf + 1) * HPB):
                        last = nc.vector.tensor_scalar(x1[:, i, :], x1[:, i, :], mean_var[:, i, 0:1], rstd[:, i:i + 1],
                                                       ALU.subtract, ALU.mult)
                    last.then_inc(x1_ready, 1)

                for i in range(HPB):
                    add_and_count(i, 0)
                statistics(HPB - 1)
                variance(0)
                add_and_count(HPB, HPB)
                normalise(0)
                for i in range(HPB + 1, NT):
                    add_and_count(i, HPB)
                statistics(NT - 1)
                variance(1)
                normalise(1)
                split_lo(turn, TURN, 0, (b + 1) * (4 * G + 2), 0, 0)
                over = lambda k: rt[:, k, :].unsqueeze(2).to_broadcast([P, NT, E])
                each = expert_m[:, :].unsqueeze(1).to_broadcast([P, NT, E])
                bank, done = full(turn, TURN, ("logits", 0))
                nc.vector.tensor_copy(logit[:, :, :].rearrange("p t e -> p (t e)"), bank[:, 0:NT * E]).then_inc(done, 1)
                own(("logits", 0))
                step(nc.vector.tensor_reduce(rt[:, 0, :], logit[:, :, :], AX.X, ALU.max))
                settle()
                nc.vector.tensor_tensor(work_a[:, :, :], logit[:, :, :], over(0), ALU.subtract).then_inc(logit_ready, 1)
                step(nc.vector.tensor_tensor(logit[:, :, :], logit[:, :, :], over(0), ALU.is_equal))
                settle()
                step(nc.vector.tensor_tensor(logit[:, :, :], logit[:, :, :], each, ALU.mult))
                settle()
                step(nc.vector.tensor_reduce(rt[:, 3, :], logit[:, :, :], AX.X, ALU.min))
                settle()
                nc.vector.tensor_tensor(onehot[:, :, :], each, over(3), ALU.is_equal).then_inc(onehot_ready, 1)
                split_lo(turn, TURN, 0, (b + 1) * (4 * G + 2), 0, 1)
                for s in range(2):
                    row_max(s, b * SCORED + SCORED)
                dve.wait_ge(gate_exp, b + 1)
                step(nc.vector.tensor_reduce(rt[:, 1, :], work_b[:, :, :], AX.X, ALU.add))
                settle()
                step(nc.vector.reciprocal(rt[:, 2, :], rt[:, 1, :]))
                bank, done = full(turn, TURN, ("pos", 0))
                nc.vector.tensor_tensor(work_a[:, :, :], onehot[:, :, :],
                                        bank[:, 0:NT * E].rearrange("p (t e) -> p t e", e=E), ALU.mult).then_inc(done, 1)
                own(("pos", 0))
                step(nc.vector.tensor_reduce(in_tiles[:, :], onehot[:, :, :].rearrange("p t e -> p e t"), AX.X, ALU.add))
                settle()
                step(nc.vector.tensor_tensor(earlier[:, :, :], earlier[:, :, :],
                                             in_tiles[:, :].unsqueeze(1).to_broadcast([P, NT, E]), ALU.add))
                step(nc.vector.tensor_reduce(rt[:, 4, :], work_a[:, :, :], AX.X, ALU.add))
                settle()
                step(nc.vector.scalar_tensor_tensor(rt[:, 5, :], rt[:, 3, :], float(C), rt[:, 4, :], ALU.mult, ALU.add))
                step(nc.vector.tensor_scalar(rt[:, 6, :], rt[:, 4, :], float(C), None, ALU.is_lt))
                step(nc.vector.tensor_scalar(rt[:, 7, :], rt[:, 4, :], float(C), FAR, ALU.is_ge, ALU.mult))
                settle()
                step(nc.vector.scalar_tensor_tensor(rt[:, 8, :], rt[:, 5, :], float(SLOTS), rt[:, 7, :], ALU.add, ALU.add))
                step(nc.vector.tensor_tensor(gate_all[:, bass.ds(b * NT, NT)], rt[:, 2, :], rt[:, 6, :], ALU.mult))
                settle()
                nc.vector.tensor_scalar(fetch_all[:, bass.ds(b * NT, NT)], rt[:, 8, :], float(SLOTS - 1), None, ALU.min
                                        ).then_inc(routed, 1)
                nc.vector.tensor_copy(send_idx[:, :], rt[:, 8, :]).then_inc(send_ready, 1)
                assert steps[1] == END_STEPS, steps

            def copy_rows(g, i):
                dve.wait_ge(ex_t_full, g * AHEAD + (i + 1))
                nc.vector.tensor_copy(ex_xT[:, i % 4, 0, :], ring[0][:, 0:C])
                nc.vector.tensor_copy(ex_xT[:, i % 4, 1, :], ring[1][:, 0:C]).then_inc(ex_t_ready, 1)

            def hidden(g, i):
                for f in range(KF):
                    dve.wait_ge(ex_s_ready, g * (AHEAD * KF) + (i * KF + f + 1))
                    nc.vector.tensor_tensor(ex_h[:, i % 4, f, :], ex_s[:, i % 4, f, :], score_ps[f][:, BANK:BANK + C],
                                            ALU.mult).then_inc(ex_h_ready[f], 1)

            def copy_outputs(g, i):
                dve.wait_ge(ex_stored[i % 4], g * (AHEAD // 4 * 16 * NB) + (i // 4 * 16 * NB + PRIMED))
                for n, (r0, nr) in enumerate(BLOCKS):
                    bank, _ = y_use(i % 2, n)
                    dve.wait_ge(ex_y_full, g * (AHEAD * NB) + (i * NB + n + 1))
                    nc.vector.tensor_copy(ex_y[0:nr, i % 4, n, :], ring[2 + bank][0:nr, 0:D]
                                          ).then_inc(ex_y_free[bank], 1)

            def couples(g, last):
                for i in range(0, AHEAD, 2):
                    for u in range(2):
                        hidden(g, i + u)
                        if not (last and i + u + 2 >= AHEAD):
                            copy_rows(g, i + u + 2)
                    for u in range(2):
                        copy_outputs(g, i + u)

            for i in range(2):
                copy_rows(0, i)
            with dve.Fori(0, E // AHEAD - 1) as g:
                couples(g, last=False)
            couples(E // AHEAD - 1, last=True)

            dve.wait_ge(x1_back, 16 * B)
            step_gate = nc.vector.tensor_scalar(half_gate[:, :], gate_all[:, :], 0.5, None, ALU.mult)
            step_gate.then_inc(gates_ready, 1)
            dve.wait_ge(gates_ready, 1)
            with dve.Fori(0, LAST) as g:
                steps[0] = dve.snap(B * END_STEPS + g * (2 * 3))
                steps[1] = 0
                for u in range(2):
                    n = g * 2 + u
                    half_ = slice(u * NL, (u + 1) * NL)
                    dve.wait_ge(fetched[u], (g + 1) * (16 * NL))
                    for i in range(NL):
                        last = nc.vector.scalar_tensor_tensor(
                            last_y[:, u * NL + i, :], last_y[:, u * NL + i, :], half_gate[:, bass.ds(n * NL + i, 1)],
                            x1_all[:, bass.ds(n * NL + i, 1), :].rearrange("p a d -> p (a d)"), ALU.mult, ALU.add)
                    step(last)
                    settle()
                    for i in range(NL):
                        last = nc.vector.bn_stats(stat6[:, u * NL + i, :], last_y[:, u * NL + i, :])
                    step(last)
                    settle(alone=True)
                    for i in range(NL):
                        last = nc.vector.bn_aggr(mean_var[:, u * NL + i, :], stat6[:, u * NL + i, :])
                    step(last)
                    settle()
                    nc.vector.tensor_scalar(var_eps[:, half_], mean_var[:, half_, 1], EPS / 4, None, ALU.add
                                            ).then_inc(var_ready, 1)
                    dve.wait_ge(rstd_ready, n + (2 * B + 1))
                    dve.wait_ge(last_ready[u], g + PRIMED)
                    nc.vector.scalar_tensor_tensor(shift[:, half_], mean_var[:, half_, 0], -1.0, rstd[:, half_],
                                                   ALU.mult, ALU.mult).then_inc(shift_ready, 1)


_INS = ["L0_attn_x_bld", "L0_attn_Wq", "L0_attn_Wkv_down", "L0_attn_Wk_up", "L0_attn_Wv_up", "L0_attn_Wout",
        "L0_ffn_w_router", "L0_ffn_w_gate", "L0_ffn_w_up", "L0_ffn_w_down"]
_OUT = "layer_out"


def kernel(**inputs):
    import concourse.bacc as bacc
    from concourse.bass_utils import run_bass_kernel_spmd

    nc = bacc.Bacc("TRN2", target_bir_lowering=False, num_devices=1)
    arrays, aps = {}, []
    for name in _INS:
        a = np.ascontiguousarray(inputs[name])
        arrays["in_" + name] = a
        aps.append(nc.dram_tensor("in_" + name, a.shape, mybir.dt.from_np(a.dtype), kind="ExternalInput").ap())
    aps.append(nc.dram_tensor(_OUT, inputs["L0_attn_x_bld"].shape, F32, kind="ExternalOutput").ap())
    build_layer(nc, *aps)
    result = run_bass_kernel_spmd(nc, [arrays], core_ids=[0])
    return result.results[0][_OUT]
```
